# Optimizing a Trainium2 kernel written in Bass

```python
import numpy as np
import jax
import jax.numpy as jnp

def _softmax(x, axis=-1):
    return jax.nn.softmax(x, axis=axis)

def _gelu(x):
    return jax.nn.gelu(x, approximate=True)

def _silu(x):
    return jax.nn.silu(x)

def _sigmoid(x):
    return jax.nn.sigmoid(x)

def _layernorm(x, axis=-1, eps=1e-05):
    m = jnp.mean(x, axis=axis, keepdims=True)
    v = jnp.var(x, axis=axis, keepdims=True)
    return (x - m) / jnp.sqrt(v + eps)

def _scatter_add(tgt, idx, src, axis=0):
    return tgt.at[idx].add(src)

def _segment_sum(src, seg, n):
    return jax.ops.segment_sum(src, seg, n)
kernel_name = 'mk_flamingo_gated_d1_seqx_r8_fe298c'

def setup_inputs(seed: int=0):
    np.random.seed(seed)
    _w = jnp.asarray

    def _rec_inputs():
        import jax
        import jax.numpy as jnp
        _rk = jax.random.key(seed)
        x = -0.0003929 + 0.9999 * jax.random.normal(jax.random.fold_in(_rk, 1), (32, 56, 256), jnp.float32)
        _lenS = 56 - jax.random.randint(jax.random.fold_in(_rk, 7), (32,), 0, max(1, 56 // 4) + 1, jnp.int32)
        _lenS2 = 1500 - jax.random.randint(jax.random.fold_in(_rk, 8), (32,), 0, max(1, 1500 // 4) + 1, jnp.int32)
        _ctx_2048P = jax.random.normal(jax.random.fold_in(_rk, 11), (32, 16, 256), jnp.float32)
        _ctx_2048c = jax.random.dirichlet(jax.random.fold_in(_rk, 511), 0.3 * jnp.ones((16,), jnp.float32), (32, 1500))
        _ctx_2048t = jnp.einsum('bsk,bkd->bsd', _ctx_2048c, _ctx_2048P)
        _ctx_2048t = _ctx_2048t * jax.lax.rsqrt(jnp.mean(jnp.square(_ctx_2048t)) + 1e-12) * 0.953939
        ctx_2048 = -0.000514642 + 1.00011 * (_ctx_2048t + 0.3 * jax.random.normal(jax.random.fold_in(_rk, 611), (32, 1500, 256), jnp.float32))
        _g = jax.random.normal(jax.random.fold_in(_rk, 9001), (2, 1), jnp.float32)
        _g = jnp.sign(_g) * jnp.maximum(jnp.abs(_g), 1.0) + (_g == 0) * 1.0
        g_xattn = _g[0]
        g_ffn = _g[1]
        return (x, ctx_2048, g_xattn, g_ffn)
    x, ctx_2048, g_xattn, g_ffn = _rec_inputs()

    def _L0_xattn_setup():
        import jax, jax.numpy as jnp
        import numpy as np
        DIM = 256
        NHEADS = 32
        HEAD_DIM = DIM // NHEADS
        EPS = 1e-06

        def _rmsnorm(t):
            return t * jax.lax.rsqrt(jnp.mean(t * t, axis=-1, keepdims=True) + EPS)
        key = jax.random.key(seed)
        kx, kc, kq, kk, kv = jax.random.split(key, 5)
        x = jax.random.normal(kx, (2, 512, DIM), dtype=jnp.float32)
        context = jax.random.normal(kc, (2, 64, DIM), dtype=jnp.float32)
        std = 0.02
        Wq = jax.random.normal(kq, (DIM, DIM), dtype=jnp.float32) * std
        Wk = jax.random.normal(kk, (DIM, DIM), dtype=jnp.float32) * std
        Wv = jax.random.normal(kv, (DIM, DIM), dtype=jnp.float32) * std
        return {'x': x, 'context': context, 'Wq': Wq, 'Wk': Wk, 'Wv': Wv}
    _L0_xattn_all = _L0_xattn_setup()
    _L0_xattn_in = {k: v for k, v in _L0_xattn_all.items() if k in ('Wq', 'Wk', 'Wv')}
    del _L0_xattn_all

    def _L0_ffn_setup():
        import jax, jax.numpy as jnp
        import numpy as np
        import math
        N_EMBD = 256
        N_HEAD = 16
        HEAD_DIM = N_EMBD // N_HEAD
        B, T = (2, 256)
        key = jax.random.key(seed)
        k1, k2, k3 = jax.random.split(key, 3)
        x = jax.random.normal(k1, (B, T, N_EMBD), dtype=jnp.float32)
        W_gate = jax.random.normal(k2, (N_HEAD, N_EMBD), dtype=jnp.float32) * 0.02
        W_qkv = jax.random.normal(k3, (3 * N_EMBD, N_EMBD), dtype=jnp.float32) * 0.02
        return {'x': x, 'W_gate': W_gate, 'W_qkv': W_qkv}
    _L0_ffn_all = _L0_ffn_setup()
    _L0_ffn_in = {k: v for k, v in _L0_ffn_all.items() if k in ('W_gate', 'W_qkv')}
    del _L0_ffn_all
    return {'x': x, 'ctx_2048': ctx_2048, 'g_xattn': g_xattn, 'g_ffn': g_ffn, 'L0_xattn_Wq': _L0_xattn_in['Wq'], 'L0_xattn_Wk': _L0_xattn_in['Wk'], 'L0_xattn_Wv': _L0_xattn_in['Wv'], 'L0_ffn_W_gate': _L0_ffn_in['W_gate'], 'L0_ffn_W_qkv': _L0_ffn_in['W_qkv']}

def reference(x, ctx_2048, g_xattn, g_ffn, L0_xattn_Wq, L0_xattn_Wk, L0_xattn_Wv, L0_ffn_W_gate, L0_ffn_W_qkv):
    import jax
    import jax.numpy as jnp

    def _L0_xattn_ref(x, context, Wq, Wk, Wv):
        import jax, jax.numpy as jnp
        import numpy as np
        DIM = 256
        NHEADS = 32
        HEAD_DIM = DIM // NHEADS
        EPS = 1e-06

        def _rmsnorm(t):
            return t * jax.lax.rsqrt(jnp.mean(t * t, axis=-1, keepdims=True) + EPS)
        b, n, _ = x.shape
        m = context.shape[1]
        q = x @ Wq.T
        k_raw = context @ Wk.T
        v_raw = context @ Wv.T
        q = q.reshape(b, n, NHEADS, HEAD_DIM).transpose(0, 2, 1, 3)
        kv = jnp.concatenate([k_raw, v_raw], axis=-1)
        kv = kv.reshape(b, m, NHEADS, HEAD_DIM, 2)
        k = kv[..., 0].transpose(0, 2, 1, 3)
        v = kv[..., 1].transpose(0, 2, 1, 3)
        q = _rmsnorm(q)
        k = _rmsnorm(k)
        scale = HEAD_DIM ** (-0.5)
        scores = jnp.einsum('bhnd,bhmd->bhnm', q, k) * scale
        attn = jax.nn.softmax(scores, axis=-1)
        out = jnp.einsum('bhnm,bhmd->bhnd', attn, v)
        return out.transpose(0, 2, 1, 3).reshape(b, n, NHEADS * HEAD_DIM)

    def _L0_ffn_ref(x, W_gate, W_qkv):
        import jax, jax.numpy as jnp
        import numpy as np
        import math
        N_EMBD = 256
        N_HEAD = 16
        HEAD_DIM = N_EMBD // N_HEAD
        B, T = (2, 256)
        Bb, Tt, C = x.shape
        H, hd = (N_HEAD, HEAD_DIM)
        gating = jax.nn.softmax(x @ W_gate.T, axis=-1)
        idx = jnp.argmax(gating, axis=-1)
        indicator = jax.nn.one_hot(idx, H, dtype=gating.dtype)
        top1_val = jnp.max(gating, axis=-1, keepdims=True)
        gating_top1 = indicator * top1_val
        qkv = x @ W_qkv.T
        q, k, v = jnp.split(qkv, 3, axis=-1)
        k = k.reshape(Bb, Tt, H, hd)
        v = v.reshape(Bb, Tt, H, hd)
        k_shared = jnp.einsum('bth,bthd->btd', indicator, k)
        v_shared = jnp.einsum('bth,bthd->btd', gating_top1, v)
        q = q.reshape(Bb, Tt, H, hd).transpose(0, 2, 1, 3)
        att = jnp.einsum('bhqd,bkd->bhqk', q, k_shared) * (1.0 / math.sqrt(hd))
        causal = jnp.tril(jnp.ones((Tt, Tt), dtype=bool))
        att = jnp.where(causal[None, None, :, :], att, -jnp.inf)
        att = jax.nn.softmax(att, axis=-1)
        y = jnp.einsum('bhqk,bkd->bhqd', att, v_shared)
        y = y.transpose(0, 2, 1, 3).reshape(Bb, Tt, C)
        return y
    x = x + jnp.tanh(g_xattn[0]) * _L0_xattn_ref(_layernorm(x, axis=-1), ctx_2048, L0_xattn_Wq, L0_xattn_Wk, L0_xattn_Wv)
    x = x + jnp.tanh(g_ffn[0]) * _L0_ffn_ref(_layernorm(x, axis=-1), L0_ffn_W_gate, L0_ffn_W_qkv)
    return x

_drawn_inputs = setup_inputs


def setup_inputs(seed=0):
    import zlib

    import numpy as np

    out = dict(_drawn_inputs(seed))
    spreads = {}
    factors = {'L0_ffn_W_gate': 3.874, 'L0_ffn_W_qkv': 3.272}
    for name, (base, spread) in spreads.items():
        noise = np.random.default_rng([zlib.crc32(name.encode()), seed]).standard_normal(out[name].shape)
        drawn = base * np.exp(spread * noise) if base else spread * noise
        out[name] = jnp.asarray(drawn.astype(out[name].dtype))
    for name, factor in factors.items():
        out[name] = (out[name] * factor).astype(out[name].dtype)
    return out
```

```python
from contextlib import ExitStack

import concourse.bass as bass
from concourse import mybir

F32 = mybir.dt.float32
F32R = mybir.dt.float32r
F16 = mybir.dt.float16
BF16 = mybir.dt.bfloat16
ALU = mybir.AluOpType
ACT = mybir.ActivationFunctionType
AX = mybir.AxisListType

P = 128
B, N, D = 32, 56, 256
M = 1500
H, DH = 32, 8
FH, FD = 16, 16
TILES = 12
MT = M // TILES
PAIRS = B // 2
HALF = 64
IC = D // P
G = 8
TRI = (H + 2) // 3
VW = DH + 1
PAIR_TILES = 2 * TILES
LN_EPS, RMS_EPS = 1e-5, 1e-6
MASKED = -3.0e38


def gated_attention_kernel(nc, x, ctx_in, g_xattn, g_ffn, wq, wk, wv, w_gate, w_qkv, out):
    with ExitStack() as stack:
        def sb(name, shape, dt=F32):
            return stack.enter_context(nc.sbuf_tensor(name, shape, dt))

        def psum(name, shape):
            return stack.enter_context(nc.psum_tensor(name, shape, F32))

        def sem(name):
            return stack.enter_context(nc.semaphore(name))

        S = psum("S", [P, 4, 512])
        PV = psum("PV", [P, 512])
        Y = psum("Y", [P, 2, 512])
        X = psum("X", [P, 512])
        x_ctx = X[:, 0:256].rearrange("p (c m) -> p c m", c=IC)
        x_key = X[:, 256:512].bitcast(F16).rearrange("p (c m) -> p c m", c=4)

        ident = sb("ident", [P, P])
        ident16 = sb("ident16", [P, P], F16)
        mask4 = sb("mask4", [P, 4])
        mask_q = sb("mask_q", [P, 4, N], F16)
        mask8 = sb("mask8", [P, 8])
        causal = sb("causal", [HALF, HALF], BF16)
        spread = sb("spread", [HALF, 8, N], BF16)
        gates = sb("gates", [P, 2])
        tg = sb("tg", [P, 2])
        wn_kv = sb("wn_kv", [P, 2, 2, D])
        wn_q = sb("wn_q", [P, 2, D])
        wn_qkv = sb("wn_qkv", [P, 6, D])
        wn_g = sb("wn_g", [FH, D])
        w_hi = sb("w_hi", [P, IC, 2, H, DH], F32R)
        w_lo = sb("w_lo", [P, IC, 2, H, DH], F32R)
        wq_t = sb("wq_t", [P, IC, D])
        wqkv_t = sb("wqkv_t", [P, IC, 3 * D])
        wg_t = sb("wg_t", [P, IC, FH])
        xs = sb("xs", [P, PAIRS, D])
        q_t = sb("q_t", [P, G, PAIRS + 1, P], F16)

        CH = 4
        stats = sb("stats", [P, 2, PAIRS, 6])
        mv = sb("mv", [P, 2, PAIRS, 2])
        ve = sb("ve", [P, 2, PAIRS])
        vln = sb("vln", [P, 2, PAIRS])
        rst = sb("rst", [P, 2, PAIRS])
        nt = sb("nt", [P, CH * H])
        xn = sb("xn", [P, CH, D])
        xn_t = sb("xn_t", [P, CH, IC, P])
        q_sb = sb("q_sb", [P, CH * H, DH])
        q_sq = sb("q_sq", [P, CH * H, DH])
        q_ms = sb("q_ms", [P, CH * H])
        q_ln = sb("q_ln", [P, CH * H])
        q_r = sb("q_r", [P, CH * H])
        q4 = sb("q4", [P, CH, G, 4, 32], F16)

        cx = sb("cx", [P, 2, TILES, D])
        cth = sb("cth", [P, 2, IC, P], F32R)
        ctl = sb("ctl", [P, 2, IC, P], F32R)
        v9 = sb("v9", [P, 4, 33 * VW + 8])
        ksq = sb("ksq", [P, 2, H, DH])
        kms = sb("kms", [P, 2, H])
        kme = sb("kme", [P, 2, H])
        kln = sb("kln", [P, 2, H])
        kr0 = sb("kr0", [P, 2, H])
        kmh = sb("kmh", [P, H])
        kn1 = sb("kn1", [P, H])
        c_eps = sb("c_eps", [P, H])
        c_half = sb("c_half", [P, H])
        c_three = sb("c_three", [P, H])
        kn2 = sb("kn2", [P, H])
        kn3 = sb("kn3", [P, H])
        kr = sb("kr", [P, 2, H])
        khat = sb("khat", [P, H, DH])
        kp = sb("kp", [P, 2, G, 2, 32], F16)
        kt = sb("kt", [P, G, P], F16)
        q_bd = sb("q_bd", [P, 2, G, 4, N], F16)
        prob = sb("prob", [P, 2, H * N])
        pvs = sb("pvs", [P, 504])
        rden = sb("rden", [P, H])
        rdg = sb("rdg", [P, H])
        att = sb("att", [P, H, DH])

        xn2 = sb("xn2", [P, D])
        xt2 = sb("xt2", [P, IC, P])
        qt2 = sb("qt2", [P, 2, P])
        gmax = sb("gmax", [P, 1])
        gdif = sb("gdif", [P, FH])
        gexp = sb("gexp", [P, FH])
        gsum = sb("gsum", [P, 1])
        top1 = sb("top1", [P, 1])
        first = sb("first", [P, FH])
        gkey = sb("gkey", [P, FH])
        gkmax = sb("gkmax", [P, 1])
        pick = sb("pick", [P, FH])
        kvm = sb("kvm", [P, 2, FH, FD])
        kvs = sb("kvs", [P, 2, FD])
        ks_rep = sb("ks_rep", [P, 8, FD])
        ks_t = sb("ks_t", [P, P])
        ks_bd = sb("ks_bd", [P, 2, 8, N])
        vsh = sb("vsh", [P, FD])
        vs_bd = sb("vs_bd", [P, 2, 2, FD + 1])
        smax = sb("smax", [P, FH])
        sdif = sb("sdif", [P, FH, N])
        pr = sb("pr", [P, FH, HALF])
        pt = sb("pt", [P, 8, P])
        ry = sb("ry", [P, FH])
        yo = sb("yo", [P, FH, FD])

        s_mem, s_id, s_const, s_ld, s_wt, s_wc, s_tanh = map(sem, (
            "s_mem", "s_id", "s_const", "s_ld", "s_wt", "s_wc", "s_tanh"))
        s_vz = sem("s_vz")
        s_dc = sem("s_dc")
        ln_stat, ln_agg, ln_ve, ln_ln, ln_r0, ln_x = map(sem, (
            "ln_stat", "ln_agg", "ln_ve", "ln_ln", "ln_r0", "ln_x"))
        nw = sem("nw")
        q_tr, q_te, q_mm, q_cp, q_sqd, q_msd, q_lnd, q_r0, q_hat, q_hi, q_lo, q_t4, q_done = map(sem, (
            "q_tr", "q_te", "q_mm", "q_cp", "q_sqd", "q_msd", "q_lnd", "q_r0", "q_hat", "q_hi", "q_lo", "q_t4",
            "q_done"))
        ctx_loaded = [sem("ctx_loaded0"), sem("ctx_loaded1")]
        t1_done, cth_ready, ctl_ready, proj_done, sq_done, ms_done, me_done, kln_done, r0_done = map(sem, (
            "t1_done", "cth_ready", "ctl_ready", "proj_done", "sq_done", "ms_done", "me_done", "kln_done",
            "r0_done"))
        newton, khat_done, hi_done, lo_done, t2_done, kt_ready = map(sem, (
            "newton", "khat_done", "hi_done", "lo_done", "t2_done", "kt_ready"))
        sca_done, scb_done, expa_done, expb_done, qbd_ready = map(sem, (
            "sca_done", "scb_done", "expa_done", "expb_done", "qbd_ready"))
        pv_done, pvs_ready, sel_done, pv_free, den_done, rdg_done, x1_done = map(sem, (
            "pv_done", "pvs_ready", "sel_done", "pv_free", "den_done", "rdg_done", "x1_done"))

        f_xn, f_t1, f_xt, f_proj, f_gate, f_qt = map(sem, (
            "f_xn", "f_t1", "f_xt", "f_proj", "f_gate", "f_qt"))
        f_gdif, f_gexp, f_kv, f_rep, f_t2, f_kst, f_ksb, f_vsb, f_att, f_smax, f_sdif, f_exp = map(sem, (
            "f_gdif", "f_gexp", "f_kv", "f_rep", "f_t2", "f_kst", "f_ksb", "f_vsb", "f_att", "f_smax", "f_sdif",
            "f_exp"))
        f_t3, f_pt, f_y, f_ry, f_out, f_stored = map(sem, ("f_t3", "f_pt", "f_y", "f_ry", "f_out", "f_stored"))

        def ffn_store(sp):
            with sp.Fori(0, PAIRS) as t:
                sp.wait_ge(f_out, t + 1)
                for j in range(2):
                    sp.dma_start(out[bass.ds(t * 2 + j, 1)].rearrange("o n d -> (o n) d"),
                                 xs[HALF * j:HALF * j + N, bass.ds(t, 1)].rearrange("p o d -> p (o d)")
                                 ).then_inc(f_stored, 16)
            sp.wait_ge(f_stored, 16 * B)

        def ffn_gpsimd(pool):
            with pool.Fori(0, PAIRS) as t:
                pool.wait_ge(f_kst, t + 1)
                nc.gpsimd.tensor_tensor(
                    ks_bd[:], ks_t[:].rearrange("p (j o k) -> p j o k", j=2, o=1)[:, :, :, 0:N]
                    .broadcast_to((P, 2, 8, N)),
                    mask8[:].rearrange("p (j h o) -> p j h o", j=1, o=1).broadcast_to((P, 2, 8, N)), ALU.mult
                ).then_inc(f_ksb, 1)

        def norm_estimate(act, which):
            act.wait_ge(ln_ve, which + 1)
            nc.scalar.activation(vln[:, which], ve[:, which], ACT.Ln).then_inc(ln_ln, 1)
            act.wait_ge(ln_ln, which + 1)
            nc.scalar.activation(rst[:, which], vln[:, which], ACT.Exp, scale=-0.5).then_inc(ln_r0, 1)

        def newton_step(dve, y, arg, tmp, base):
            nc.vector.tensor_tensor(tmp, y, y, ALU.mult).then_inc(nw, 1)
            dve.wait_ge(nw, base + 1)
            nc.vector.scalar_tensor_tensor(tmp, tmp, -0.5, arg, ALU.mult, ALU.mult).then_inc(nw, 1)
            dve.wait_ge(nw, base + 2)
            nc.vector.scalar_tensor_tensor(y, tmp, 1.5, y, ALU.add, ALU.mult).then_inc(nw, 1)
            dve.wait_ge(nw, base + 3)

        def layer_norm(dve, which, nw_base):
            for t in range(PAIRS):
                nc.vector.bn_stats(stats[:, which, t], xs[:, t]).then_inc(ln_stat, 1)
            for t in range(PAIRS):
                dve.wait_ge(ln_stat, which * PAIRS + t + 1)
                nc.vector.bn_aggr(mv[:, which, t], stats[:, which, t]).then_inc(ln_agg, 1)
            dve.wait_ge(ln_agg, (which + 1) * PAIRS)
            nc.vector.tensor_scalar(ve[:, which], mv[:, which, :, 1], LN_EPS, None, ALU.add).then_inc(ln_ve, 1)
            dve.wait_ge(ln_r0, which + 1)
            newton_step(dve, rst[:, which], ve[:, which], nt[:, 0:PAIRS], nw_base)

        def normed(dst, which, t):
            tile = bass.ds(t, 1)
            return nc.vector.tensor_scalar(
                dst, xs[:, tile].rearrange("p o d -> p (o d)"), mv[:, which, tile, 0], rst[:, which, tile],
                ALU.subtract, ALU.mult)

        def ffn_scalar(act):
            norm_estimate(act, 1)
            with act.Fori(0, PAIRS) as t:
                act.wait_ge(f_t1, t + 1)
                nc.scalar.copy(xt2[:], x_ctx).then_inc(f_xt, 1)
                act.wait_ge(f_proj, t + 1)
                nc.scalar.copy(qt2[:], Y[:, 1, 0:256].rearrange("p (c m) -> p c m", c=2)).then_inc(f_qt, 1)
                act.wait_ge(f_gdif, t + 1)
                nc.scalar.activation(gexp[:], gdif[:], ACT.Exp).then_inc(f_gexp, 1)
                act.wait_ge(f_t2, t + 1)
                nc.scalar.copy(ks_t[:], X[:, 256:384]).then_inc(f_kst, 1)
                act.wait_ge(f_sdif, t + 1)
                nc.scalar.activation(pr[:, :, 0:N], sdif[:], ACT.Exp, scale=FD ** -0.5).then_inc(f_exp, 1)
                act.wait_ge(f_t3, t + 1)
                nc.scalar.copy(pt[:].rearrange("p (a h) q -> p a (h q)", a=2), S[:, 2:4]).then_inc(f_pt, 1)

        def ffn_vector(dve):
            dve.wait_ge(x1_done, B)
            layer_norm(dve, 1, 3 + 3 * CH)
            with dve.Fori(0, PAIRS) as t:
                row = xs[:, bass.ds(t, 1)].rearrange("p o d -> p (o d)")
                normed(xn2[:], 1, t).then_inc(f_xn, 1)
                logits = Y[:, 1, 256:256 + FH]
                dve.wait_ge(f_proj, t + 1)
                dve.wait_ge(f_qt, t + 1)
                nc.vector.tensor_reduce(gmax[:], logits, AX.X, ALU.max).then_inc(f_gate, 1)
                dve.wait_ge(f_gate, t * 8 + 1)
                nc.vector.tensor_scalar(gdif[:], logits, gmax[:], None, ALU.subtract).then_inc(f_gdif, 1)
                nc.vector.scalar_tensor_tensor(gkey[:], logits, gmax[:], first[:], ALU.is_equal, ALU.mult
                                               ).then_inc(f_gate, 1)
                dve.wait_ge(f_gate, t * 8 + 2)
                nc.vector.tensor_reduce(gkmax[:], gkey[:], AX.X, ALU.max).then_inc(f_gate, 1)
                dve.wait_ge(f_gate, t * 8 + 3)
                nc.vector.tensor_scalar(pick[:], gkey[:], gkmax[:], None, ALU.is_equal).then_inc(f_gate, 1)
                dve.wait_ge(f_gate, t * 8 + 4)
                nc.vector.tensor_tensor(kvm[:], Y[:, 0].rearrange("p (e h d) -> p e h d", e=2, h=FH),
                                        pick[:].rearrange("p (e h o) -> p e h o", e=1, o=1)
                                        .broadcast_to((P, 2, FH, FD)), ALU.mult).then_inc(f_gate, 1)
                dve.wait_ge(f_gate, t * 8 + 5)
                nc.vector.tensor_reduce(kvs[:], kvm[:].rearrange("p e h d -> p e d h"), AX.X, ALU.add
                                        ).then_inc(f_kv, 1)
                dve.wait_ge(f_kv, t + 1)
                nc.vector.tensor_copy(ks_rep[:], kvs[:, 0:1].broadcast_to((P, 8, FD))).then_inc(f_rep, 1)
                dve.wait_ge(f_gexp, t + 1)
                nc.vector.tensor_reduce(gsum[:], gexp[:], AX.X, ALU.add).then_inc(f_gate, 1)
                dve.wait_ge(f_gate, t * 8 + 6)
                nc.vector.reciprocal(top1[:], gsum[:]).then_inc(f_gate, 1)
                dve.wait_ge(f_gate, t * 8 + 7)
                nc.vector.tensor_scalar(vsh[:], kvs[:, 1], top1[:], None, ALU.mult).then_inc(f_gate, 1)
                dve.wait_ge(f_gate, t * 8 + 8)
                for j in range(2):
                    for h in range(2):
                        tail = nc.vector.tensor_copy(vs_bd[HALF * h:HALF * h + HALF, j, h, 0:FD],
                                                     vsh[HALF * j:HALF * j + HALF])
                tail.then_inc(f_vsb, 1)
                scores = S[:, 0:2, 0:8 * N].rearrange("p c (h k) -> p c h k", h=8)
                dve.wait_ge(f_att, t + 1)
                nc.vector.tensor_reduce(smax[:].rearrange("p (c h) -> p c h", c=2), scores, AX.X, ALU.max
                                        ).then_inc(f_smax, 1)
                dve.wait_ge(f_smax, t + 1)
                nc.vector.tensor_tensor(sdif[:].rearrange("p (c h) k -> p c h k", c=2), scores,
                                        smax[:].rearrange("p (c h o) -> p c h o", c=2, o=1)
                                        .broadcast_to((P, 2, 8, N)), ALU.subtract).then_inc(f_sdif, 1)
                got = PV[:, 0:FH * (FD + 1)].rearrange("p (h c) -> p h c", c=FD + 1)
                dve.wait_ge(f_y, t + 1)
                nc.vector.reciprocal(ry[:], got[:, :, FD]).then_inc(f_ry, 1)
                dve.wait_ge(f_ry, t * 3 + 1)
                nc.vector.tensor_scalar(ry[:], ry[:], tg[:, 1:2], None, ALU.mult).then_inc(f_ry, 1)
                dve.wait_ge(f_ry, t * 3 + 2)
                nc.vector.tensor_tensor(yo[:], got[:, :, 0:FD], ry[:].rearrange("p (h o) -> p h o", o=1)
                                        .broadcast_to((P, FH, FD)), ALU.mult).then_inc(f_ry, 1)
                dve.wait_ge(f_ry, t * 3 + 3)
                nc.vector.tensor_tensor(row, row, yo[:].rearrange("p h d -> p (h d)"), ALU.add).then_inc(f_out, 1)

        def ffn_tensor(pe):
            pe.wait_ge(kt_ready, B * TILES + 1)
            pe.wait_ge(x1_done, B)
            with pe.Fori(0, PAIRS) as t:
                pe.wait_ge(f_xn, t + 1)
                for c in range(IC):
                    tail = nc.tensor.transpose(x_ctx[:, c], xn2[:, c * P:c * P + P], ident[:])
                tail.then_inc(f_t1, 1)
                pe.wait_ge(f_xt, t + 1)
                for c in range(IC):
                    nc.tensor.matmul(Y[:, 1, 256:256 + FH], xt2[:, c], wg_t[:, c], start=(c == 0),
                                     stop=(c == IC - 1))
                for o in range(2):
                    for c in range(IC):
                        nc.tensor.matmul(Y[:, 1, o * P:o * P + P], wqkv_t[:, c, o * P:o * P + P], xt2[:, c],
                                         start=(c == 0), stop=(c == IC - 1))
                for c in range(IC):
                    tail = nc.tensor.matmul(Y[:, 0], xt2[:, c], wqkv_t[:, c, D:3 * D], start=(c == 0),
                                            stop=(c == IC - 1))
                tail.then_inc(f_proj, 1)
                pe.wait_ge(f_rep, t + 1)
                nc.tensor.transpose(X[:, 256:384], ks_rep[:].rearrange("p h d -> p (h d)"), ident[:]
                                    ).then_inc(f_t2, 1)
                pe.wait_ge(f_qt, t + 1)
                pe.wait_ge(f_ksb, t + 1)
                for c in range(2):
                    for j in range(2):
                        dst = S[HALF * j:HALF * j + HALF, c, 0:8 * N]
                        nc.tensor.matmul(dst, qt2[:, c, HALF * j:HALF * j + HALF],
                                         ks_bd[:, j].rearrange("p h k -> p (h k)"), start=True, stop=False)
                        tail = nc.tensor.matmul(dst, causal[:], spread[:].rearrange("p h k -> p (h k)"),
                                                start=False, stop=True)
                tail.then_inc(f_att, 1)
                pe.wait_ge(f_exp, t + 1)
                for h in range(8):
                    tail = nc.tensor.transpose(S[:, 2 + h // 4, (h % 4) * P:(h % 4 + 1) * P],
                                               pr[:, 2 * h:2 * h + 2].rearrange("p a k -> p (a k)"), ident[:])
                tail.then_inc(f_t3, 1)
                pe.wait_ge(f_pt, t + 1)
                pe.wait_ge(f_vsb, t + 1)
                for h in range(8):
                    for j in range(2):
                        tail = nc.tensor.matmul(
                            PV[HALF * j:HALF * j + HALF, h * 2 * (FD + 1):(h + 1) * 2 * (FD + 1)],
                            pt[:, h, HALF * j:HALF * j + HALF], vs_bd[:, j].rearrange("p h d -> p (h d)"),
                            start=True, stop=True)
                tail.then_inc(f_y, 1)

        block = stack.enter_context(nc.Block())
        N_LOADS = 9

        @block.sync
        def _(sp):
            sp.wait_ge(s_mem, 1)
            for j in range(2):
                sp.dma_start(xs[HALF * j:HALF * j + N], x.rearrange("(p j) n d -> j n p d", j=2)[j]).then_inc(s_ld, 16)
            sp.dma_start(wn_q[:], wq.rearrange("(r p) i -> p r i", p=P)).then_inc(s_ld, 16)
            sp.dma_start(wn_kv[:, 0], wk.rearrange("(r p) i -> p r i", p=P)).then_inc(s_ld, 16)
            sp.dma_start(wn_kv[:, 1], wv.rearrange("(r p) i -> p r i", p=P)).then_inc(s_ld, 16)
            sp.dma_start(wn_qkv[:], w_qkv.rearrange("(r p) i -> p r i", p=P)).then_inc(s_ld, 16)
            sp.dma_start(wn_g[:], w_gate).then_inc(s_ld, 16)
            sp.dma_start(gates[:, 0:1], g_xattn.rearrange("(o a) -> o a", o=1).broadcast_to((P, 1))).then_inc(s_ld, 16)
            sp.dma_start(gates[:, 1:2], g_ffn.rearrange("(o a) -> o a", o=1).broadcast_to((P, 1))).then_inc(s_ld, 16)
            rows = ctx_in.rearrange("b (p t) d -> b p t d", t=TILES)
            for b in range(2):
                sp.dma_start(cx[0:MT, b], rows[b]).then_inc(ctx_loaded[b], 16)
            with sp.Fori(0, PAIRS - 1) as pair:
                for b in range(2):
                    sp.wait_ge(t1_done, pair * PAIR_TILES + TILES * (b + 1))
                    sp.dma_start(cx[0:MT, b], rows[bass.ds(pair * 2 + (2 + b), 1)].rearrange("o p t d -> (o p) t d")
                                 ).then_inc(ctx_loaded[b], 16)
            sp.wait_ge(t1_done, B * TILES - TILES)
            sp.dma_start(cx[0:MT, 0], rows[0]).then_inc(ctx_loaded[0], 16)
            ffn_store(sp)

        @block.gpsimd
        def _(pool):
            nc.gpsimd.memset(c_eps[:], RMS_EPS)
            nc.gpsimd.memset(c_half[:], -0.5)
            nc.gpsimd.memset(c_three[:], 1.5)
            nc.gpsimd.memset(ident[:], 0.0).then_inc(s_id, 1)
            pool.wait_ge(s_id, 1)
            nc.gpsimd.affine_select(out=ident[:], in_=ident[:], compare_op=ALU.not_equal, fill=1.0, base=0,
                                    pattern=[[-1, P]], channel_multiplier=1).then_inc(s_id, 1)
            nc.gpsimd.memset(causal[:], 0.0).then_inc(s_id, 1)
            pool.wait_ge(s_id, 3)
            nc.gpsimd.affine_select(out=causal[:], in_=causal[:], compare_op=ALU.is_ge, fill=MASKED, base=0,
                                    pattern=[[1, HALF]], channel_multiplier=-1).then_inc(s_id, 1)

            def build_q(par, pair):
                src = q_t[:, :, bass.ds(pair, 1), HALF * par:HALF * par + N]
                nc.gpsimd.tensor_tensor(
                    q_bd[:, par], src.rearrange("p g o n -> p g o n").broadcast_to((P, G, 4, N)),
                    mask_q[:].rearrange("p (o h) n -> p o h n", o=1).broadcast_to((P, G, 4, N)),
                    ALU.mult).then_inc(qbd_ready, 1)

            def keys_rsqrt(T, k):
                pool.wait_ge(ms_done, T + 1)
                nc.gpsimd.tensor_tensor(kme[:, k % 2], kms[:, k % 2], c_eps[:], ALU.add).then_inc(me_done, 1)
                pool.wait_ge(me_done, T + 1)
                pool.wait_ge(r0_done, T + 1)
                nc.gpsimd.tensor_tensor(kmh[:], kme[:, k % 2], c_half[:], ALU.mult)
                nc.gpsimd.tensor_tensor(kn1[:], kr0[:, k % 2], kr0[:, k % 2], ALU.mult).then_inc(newton, 1)
                pool.wait_ge(newton, T * 4 + 1)
                nc.gpsimd.tensor_tensor(kn2[:], kn1[:], kmh[:], ALU.mult).then_inc(newton, 1)
                pool.wait_ge(newton, T * 4 + 2)
                nc.gpsimd.tensor_tensor(kn3[:], kn2[:], c_three[:], ALU.add).then_inc(newton, 1)
                pool.wait_ge(newton, T * 4 + 3)
                nc.gpsimd.tensor_tensor(kr[:, k % 2], kn3[:], kr0[:, k % 2], ALU.mult).then_inc(newton, 1)

            pool.wait_ge(s_const, 1)
            pool.wait_ge(q_done, CH)
            build_q(0, 0)
            for k in range(2):
                keys_rsqrt(k, k)
            with pool.Fori(0, PAIRS) as pair:
                T0 = pool.snap(pair * PAIR_TILES)
                for par in range(2):
                    for i in range(TILES):
                        t = par * TILES + i
                        keys_rsqrt(T0 + (t + 2), t + 2)
                        if i == 2:
                            build_q(1 - par, pair + par)
            ffn_gpsimd(pool)

        @block.scalar
        def _(act):
            act.wait_ge(s_ld, 16 * N_LOADS)
            nc.scalar.activation(tg[:], gates[:], ACT.Tanh).then_inc(s_tanh, 1)
            nc.scalar.preload_act_table_set("natural_log_exp_and_others")
            act.wait_ge(s_wt, 1)
            nc.scalar.copy(wq_t[:].rearrange("p c (r o) -> p c r o", r=2),
                           S[:, 2].rearrange("p (c r o) -> p c r o", c=IC, r=2)).then_inc(s_wc, 1)
            for n, bank in enumerate((S[:, 3], Y[:, 0], Y[:, 1])):
                nc.scalar.copy(wqkv_t[:, :, n * 256:n * 256 + 256].rearrange("p c (r o) -> p c r o", r=2),
                               bank.rearrange("p (c r o) -> p c r o", c=IC, r=2)).then_inc(s_wc, 1)
            nc.scalar.copy(wg_t[:], X[:, 0:IC * FH].rearrange("p (c o) -> p c o", c=IC)).then_inc(s_wc, 1)

            norm_estimate(act, 0)
            with act.Fori(0, CH) as c:
                act.wait_ge(q_tr, c + 1)
                nc.scalar.copy(xn_t[:].rearrange("p (a u) c m -> p a (u c m)", a=2), S[:, 0:2]).then_inc(q_te, 1)
                act.wait_ge(q_mm, c + 1)
                nc.scalar.activation(q_sq[:].rearrange("p (a h) d -> p a (h d)", a=2), S[:, 2:4], ACT.Square,
                                     scale=DH ** -0.5).then_inc(q_sqd, 1)
                nc.scalar.copy(q_sb[:].rearrange("p (a h) d -> p a (h d)", a=2), S[:, 2:4]).then_inc(q_cp, 1)
                act.wait_ge(q_msd, c + 1)
                nc.scalar.activation(q_ln[:], q_ms[:], ACT.Ln).then_inc(q_lnd, 1)
                act.wait_ge(q_lnd, c + 1)
                nc.scalar.activation(q_r[:], q_ln[:], ACT.Exp, scale=-0.5).then_inc(q_r0, 1)

            def v_and_squares(T, k):
                act.wait_ge(proj_done, T + 1)
                nc.scalar.copy(v9[:, k % 4, 0:H * VW].rearrange("p (h c) -> p h c", c=VW)[:, :, 0:DH],
                               Y[:, k % 2, 256:512].rearrange("p (h d) -> p h d", d=DH))
                nc.scalar.activation(ksq[:, k % 2], Y[:, k % 2, 0:256].rearrange("p (h d) -> p h d", d=DH),
                                     ACT.Square, scale=DH ** -0.5).then_inc(sq_done, 1)

            def context_hi(T, k):
                act.wait_ge(t1_done, T + 1)
                nc.scalar.copy(cth[:, k % 2], x_ctx).then_inc(cth_ready, 1)

            def keys_estimate(T, k):
                act.wait_ge(me_done, T + 1)
                nc.scalar.activation(kln[:, k % 2], kme[:, k % 2], ACT.Ln).then_inc(kln_done, 1)
                act.wait_ge(kln_done, T + 1)
                nc.scalar.activation(kr0[:, k % 2], kln[:, k % 2], ACT.Exp, scale=-0.5).then_inc(r0_done, 1)

            def exps(T, k, half, scores, done):
                act.wait_ge(scores, T + 1)
                dst = prob[0:MT, k % 2, half * 896:half * 896 + 896].rearrange("p (a n) -> p a n", a=2)
                nc.scalar.activation(dst, S[0:MT, 2 * half:2 * half + 2, 0:448], ACT.Exp,
                                     scale=DH ** -0.5).then_inc(done, 1)

            act.wait_ge(q_cp, CH)
            nc.scalar.copy(kln[:, 0], q_ln[:, 0:H]).then_inc(expa_done, 1)
            nc.scalar.copy(kln[:, 1], q_ln[:, 0:H]).then_inc(expb_done, 1)
            context_hi(0, 0)
            context_hi(1, 1)
            v_and_squares(0, 0)
            keys_estimate(0, 0)
            context_hi(2, 2)
            v_and_squares(1, 1)
            keys_estimate(1, 1)
            with act.Fori(0, PAIRS) as pair:
                T0 = act.snap(pair * PAIR_TILES)
                for par in range(2):
                    for i in range(TILES):
                        t = par * TILES + i
                        T = T0 + t
                        last = i == TILES - 1
                        if not last:
                            v_and_squares(T + 2, t + 2)
                        exps(T, t, 0, sca_done, expa_done)
                        context_hi(T + 3, t + 3)
                        if not last:
                            keys_estimate(T + 2, t + 2)
                        exps(T, t, 1, scb_done, expb_done)
                        if last:
                            act.wait_ge(pv_done, pair * 2 + (par + 1))
                            nc.scalar.copy(pvs[:], PV[:, 0:504]).then_inc(pvs_ready, 1)
                            v_and_squares(T + 2, t + 2)
                            keys_estimate(T + 2, t + 2)
            ffn_scalar(act)

        @block.vector
        def _(dve):
            nc.vector.memset(xs[:], 0.0)
            nc.vector.memset(cx[96:P], 0.0).then_inc(s_mem, 1)
            nc.vector.memset(PV[:], 1.0).then_inc(pv_free, 1)
            nc.vector.memset(v9[:], 1.0)
            nc.vector.memset(q_t[:, :, PAIRS], 0.0)
            nc.vector.memset(pr[:], 0.0)
            nc.vector.memset(vs_bd[:], 0.0).then_inc(s_vz, 1)
            dve.wait_ge(s_vz, 1)
            for h in range(2):
                nc.vector.memset(vs_bd[HALF * h:HALF * h + HALF, :, h, FD], 1.0)
            for h in range(FH):
                nc.vector.memset(first[:, h:h + 1], float(FH - h))
            dve.wait_ge(s_id, 4)
            nc.vector.tensor_copy(ident16[:], ident[:])
            nc.vector.tensor_reduce(mask4[:], ident[:].rearrange("p (q h d) -> p h q d", q=4, h=4), AX.XY,
                                    ALU.add).then_inc(s_dc, 1)
            nc.vector.tensor_reduce(mask8[:], ident[:].rearrange("p (h d) -> p h d", h=8), AX.X, ALU.add)
            nc.vector.tensor_copy(spread[:], ident[0:HALF, 0:N].rearrange("p (o k) -> p o k", o=1)
                                  .broadcast_to((HALF, 8, N)))
            dve.wait_ge(s_dc, 1)
            nc.vector.tensor_copy(mask_q[:], mask4[:].rearrange("p (h o) -> p h o", o=1).broadcast_to((P, 4, N))
                                  ).then_inc(s_const, 1)

            dve.wait_ge(s_wt, 1)
            for w in range(2):
                for c in range(IC):
                    for r in range(2):
                        src = S[:, w].rearrange("p (c r h d e) -> p c r e h d", c=IC, r=2, h=8, d=DH)[:, c, r]
                        at = w * 16 + r * 8
                        nc.vector.tensor_copy(w_hi[:, c, :, at:at + 8], src).then_inc(s_dc, 1)
            dve.wait_ge(s_dc, 9)
            for w in range(2):
                for c in range(IC):
                    for r in range(2):
                        src = S[:, w].rearrange("p (c r h d e) -> p c r e h d", c=IC, r=2, h=8, d=DH)[:, c, r]
                        at = w * 16 + r * 8
                        nc.vector.tensor_tensor(w_lo[:, c, :, at:at + 8], src,
                                                w_hi[:, c, :, at:at + 8].bitcast(F32), ALU.subtract
                                                ).then_inc(s_wc, 1)

            dve.wait_ge(s_ld, 16 * N_LOADS)
            layer_norm(dve, 0, 0)
            with dve.Fori(0, CH) as c:
                for u in range(CH):
                    normed(xn[:, u], 0, c * CH + u).then_inc(ln_x, 1)
                dve.wait_ge(q_sqd, c + 1)
                nc.vector.tensor_reduce(q_ms[:], q_sq[:], AX.X, ALU.add).then_inc(q_hat, 1)
                dve.wait_ge(q_hat, c * 3 + 1)
                nc.vector.tensor_scalar(q_ms[:], q_ms[:], RMS_EPS, None, ALU.add).then_inc(q_msd, 1)
                dve.wait_ge(q_r0, c + 1)
                newton_step(dve, q_r[:], q_ms[:], nt[:], c * 3 + 3)
                dve.wait_ge(q_cp, c + 1)
                nc.vector.tensor_tensor(q_sb[:], q_sb[:], q_r[:].rearrange("p (h o) -> p h o", o=1)
                                        .broadcast_to((P, CH * H, DH)), ALU.mult).then_inc(q_hat, 1)
                dve.wait_ge(q_hat, c * 3 + 2)
                hat = q_sb[:].rearrange("p (g o h) d -> p g o (h d)", o=1, h=4).broadcast_to((P, CH * G, 2, 32))
                q4v = q4[:].rearrange("p u g a r -> p (u g) a r")
                nc.vector.tensor_copy(q4v[:, :, 0:2], hat).then_inc(q_hat, 1)
                dve.wait_ge(q_hat, c * 3 + 3)
                nc.vector.tensor_tensor(q4v[:, :, 2:4], hat, q4v[:, :, 0:2], ALU.subtract).then_inc(q_lo, 1)
                dve.wait_ge(q_t4, c + 1)
                for u, bank in enumerate((X, Y[:, 0], Y[:, 1], S[:, 0])):
                    tail = nc.vector.tensor_copy(q_t[:, :, bass.ds(c * CH + u, 1)].rearrange("p g o m -> p g (o m)"),
                                                 bank.bitcast(F16).rearrange("p (g m) -> p g m", g=G))
                tail.then_inc(q_done, 1)

            def context_lo(T, k):
                dve.wait_ge(cth_ready, T + 1)
                nc.vector.tensor_tensor(ctl[:, k % 2], x_ctx, cth[:, k % 2].bitcast(F32), ALU.subtract
                                        ).then_inc(ctl_ready, 1)

            def keys_ms(T, k):
                dve.wait_ge(sq_done, T + 1)
                nc.vector.tensor_reduce(kms[:, k % 2], ksq[:, k % 2], AX.X, ALU.add).then_inc(ms_done, 1)

            def keys_parts(T, k):
                dve.wait_ge(newton, T * 4 + 4)
                nc.vector.tensor_tensor(khat[:], Y[:, k % 2, 0:256].rearrange("p (h d) -> p h d", d=DH),
                                        kr[:, k % 2].rearrange("p (h o) -> p h o", o=1).broadcast_to((P, H, DH)),
                                        ALU.mult).then_inc(khat_done, 1)
                dve.wait_ge(khat_done, T + 1)
                hat = khat[:].rearrange("p (g h) d -> p g (h d)", h=4)
                nc.vector.tensor_copy(kp[:, k % 2, :, 0], hat).then_inc(hi_done, 1)
                dve.wait_ge(hi_done, T + 1)
                nc.vector.tensor_tensor(kp[:, k % 2, :, 1], hat, kp[:, k % 2, :, 0], ALU.subtract
                                        ).then_inc(lo_done, 1)

            def keys_spread(T, k):
                dve.wait_ge(t2_done, T + 1)
                for odd in range(2):
                    for dst in range(2):
                        tail = nc.vector.tensor_copy(
                            kt[HALF * dst:HALF * dst + HALF].rearrange("p (c o) m -> p c o m", o=2)[:, :, odd],
                            x_key[HALF * odd:HALF * odd + HALF])
                tail.then_inc(kt_ready, 1)

            def normalise(par, pair):
                rows = slice(HALF * par, HALF * par + N)
                got = PV[rows, 0:H * VW].rearrange("p (h c) -> p h c", c=VW)
                n = pair * 2 + (par + 1)
                dve.wait_ge(sel_done, n)
                nc.vector.reciprocal(rden[rows], got[:, :, DH]).then_inc(den_done, 1)
                dve.wait_ge(den_done, n)
                nc.vector.tensor_scalar(rdg[rows], rden[rows], tg[rows, 0:1], None, ALU.mult).then_inc(rdg_done, 1)
                dve.wait_ge(rdg_done, n)
                nc.vector.tensor_tensor(att[rows], got[:, :, 0:DH], rdg[rows].rearrange("p (h o) -> p h o", o=1)
                                        .broadcast_to((N, H, DH)), ALU.mult).then_inc(pv_free, 1)
                dve.wait_ge(pv_free, n + 1)
                row = xs[rows, bass.ds(pair, 1)].rearrange("p o d -> p (o d)")
                nc.vector.tensor_tensor(row, row, att[rows].rearrange("p h d -> p (h d)"), ALU.add
                                        ).then_inc(x1_done, 1)

            dve.wait_ge(s_tanh, 1)
            context_lo(0, 0)
            context_lo(1, 1)
            keys_ms(0, 0)
            keys_parts(0, 0)
            context_lo(2, 2)
            keys_spread(0, 0)
            keys_ms(1, 1)
            keys_parts(1, 1)
            with dve.Fori(0, PAIRS) as pair:
                T0 = dve.snap(pair * PAIR_TILES)
                for par in range(2):
                    for i in range(TILES):
                        t = par * TILES + i
                        T = T0 + t
                        last = i == TILES - 1
                        if not last:
                            keys_ms(T + 2, t + 2)
                        context_lo(T + 3, t + 3)
                        keys_spread(T + 1, t + 1)
                        if last:
                            keys_ms(T + 2, t + 2)
                        keys_parts(T + 2, t + 2)
                        if last:
                            normalise(par, pair)
            ffn_vector(dve)

        @block.tensor
        def _(pe):
            pe.wait_ge(s_id, 4)
            pe.wait_ge(s_ld, 16 * N_LOADS)
            for w in range(2):
                for c in range(IC):
                    for r in range(2):
                        nc.tensor.transpose(S[:, w, (c * 2 + r) * P:(c * 2 + r + 1) * P],
                                            wn_kv[:, w, r, c * P:c * P + P], ident[:])
            for c in range(IC):
                for r in range(2):
                    nc.tensor.transpose(S[:, 2, (c * 2 + r) * P:(c * 2 + r + 1) * P], wn_q[:, r, c * P:c * P + P],
                                        ident[:])
            for n, bank in enumerate((S[:, 3], Y[:, 0], Y[:, 1])):
                for c in range(IC):
                    for r in range(2):
                        nc.tensor.transpose(bank[:, (c * 2 + r) * P:(c * 2 + r + 1) * P],
                                            wn_qkv[:, 2 * n + r, c * P:c * P + P], ident[:])
            for c in range(IC):
                tail = nc.tensor.transpose(X[:, c * FH:c * FH + FH], wn_g[:, c * P:c * P + P], ident[0:FH, 0:FH])
            tail.then_inc(s_wt, 1)
            pe.wait_ge(s_wc, 13)

            with pe.Fori(0, CH) as c:
                pe.wait_ge(ln_x, c * CH + CH)
                for u in range(CH):
                    for k in range(IC):
                        tail = nc.tensor.transpose(S[:, u // 2, ((u % 2) * IC + k) * P:((u % 2) * IC + k + 1) * P],
                                                   xn[:, u, k * P:k * P + P], ident[:])
                tail.then_inc(q_tr, 1)
                pe.wait_ge(q_te, c + 1)
                for u in range(CH):
                    for k in range(IC):
                        tail = nc.tensor.matmul(S[:, 2 + u // 2, (u % 2) * D:(u % 2) * D + D], xn_t[:, u, k],
                                                wq_t[:, k], start=(k == 0), stop=(k == IC - 1))
                tail.then_inc(q_mm, 1)
                pe.wait_ge(q_lo, c + 1)
                for u, bank in enumerate((X, Y[:, 0], Y[:, 1], S[:, 0])):
                    for g in range(G):
                        tail = nc.tensor.transpose(bank.bitcast(F16)[:, g * P:g * P + P],
                                                   q4[:, u, g].rearrange("p a r -> p (a r)"), ident16[:])
                tail.then_inc(q_t4, 1)
                pe.wait_ge(q_done, c + 1)

            def context_transpose(T, k):
                tile = k % TILES
                for c in range(IC):
                    tail = nc.tensor.transpose(x_ctx[:, c], cx[:, (k // TILES) % 2, tile, c * P:c * P + P], ident[:])
                tail.then_inc(t1_done, 1)

            def project(T, k):
                dst = Y[:, k % 2]
                steps = [(a, w, c) for a, w in ((cth, w_hi), (cth, w_lo), (ctl, w_hi)) for c in range(IC)]
                for n, (a, w, c) in enumerate(steps):
                    tail = nc.tensor.matmul(dst, a[:, k % 2, c], w[:, c].rearrange("p e h d -> p (e h d)"),
                                            start=(n == 0), stop=(n == len(steps) - 1))
                tail.then_inc(proj_done, 1)

            def key_transpose(T, k):
                for c in range(4):
                    tail = nc.tensor.transpose(x_key[:, c], kp[:, k % 2, 2 * c:2 * c + 2].rearrange(
                        "p g a r -> p (g a r)"), ident16[:])
                tail.then_inc(t2_done, 1)

            def score(par, half, done):
                for g in range(4 * half, 4 * half + 4):
                    tail = nc.tensor.matmul(S[:, g // 2, (g % 2) * 4 * N:(g % 2 + 1) * 4 * N], kt[:, g],
                                            q_bd[:, par, g].rearrange("p h n -> p (h n)"), start=True, stop=True)
                tail.then_inc(done, 1)

            def weigh(k, done=None):
                tile = k % TILES
                for j in range(TRI):
                    quad, slot = j % 4, j // 4
                    n = min(3 * N, H * N - 3 * N * j)
                    tail = nc.tensor.matmul(PV[32 * quad:32 * quad + 32, slot * 3 * N:slot * 3 * N + n],
                                            v9[0:MT, k % 4, j * 3 * VW:j * 3 * VW + 32],
                                            prob[0:MT, k % 2, j * 3 * N:j * 3 * N + n],
                                            start=(tile == 0 and slot == 0), stop=(tile == TILES - 1),
                                            skip_group_check=True)
                if done is not None:
                    tail.then_inc(done, 1)

            def select(par):
                for slot in range(3):
                    for a in range(3):
                        dst = PV[HALF * par:HALF * par + N, 0:36 * VW].rearrange("p (s i a c) -> p s a i c", s=3, i=4,
                                                                                a=3)[:, slot, a]
                        tail = nc.tensor.matmul(
                            dst, pvs[:, slot * 3 * N + a * N:slot * 3 * N + a * N + N],
                            ident[:].rearrange("p (i r) -> p i r", r=32)[:, :, a * VW:a * VW + VW],
                            start=True, stop=True)
                tail.then_inc(sel_done, 1)

            pe.wait_ge(ctx_loaded[0], 16)
            context_transpose(0, 0)
            pe.wait_ge(ctl_ready, 1)
            context_transpose(1, 1)
            project(0, 0)
            pe.wait_ge(ctl_ready, 2)
            context_transpose(2, 2)
            project(1, 1)
            pe.wait_ge(ctl_ready, 3)
            pe.wait_ge(lo_done, 1)
            key_transpose(0, 0)
            with pe.Fori(0, PAIRS) as pair:
                T0 = pe.snap(pair * PAIR_TILES)
                for par in range(2):
                    for i in range(TILES):
                        t = par * TILES + i
                        T = T0 + t
                        last = i == TILES - 1
                        if not last:
                            pe.wait_ge(khat_done, T + 1)
                            project(T + 2, t + 2)
                        if i == 0:
                            pe.wait_ge(qbd_ready, pair * 2 + (par + 1))
                        pe.wait_ge(kt_ready, T + 1)
                        pe.wait_ge(expa_done, T + 1)
                        score(par, 0, sca_done)
                        if i == TILES - 3:
                            pe.wait_ge(ctx_loaded[1 - par], (pair + (1 + par)) * 16)
                        context_transpose(T + 3, t + 3)
                        pe.wait_ge(expb_done, T + 1)
                        score(par, 1, scb_done)
                        if i == 1:
                            pe.wait_ge(pv_free, pair * 2 + (par + 1))
                        if i > 0:
                            weigh(t - 1)
                        pe.wait_ge(lo_done, T + 2)
                        pe.wait_ge(ctl_ready, T + 4)
                        key_transpose(T + 1, t + 1)
                        if last:
                            pe.wait_ge(expa_done, T + 2)
                            pe.wait_ge(expb_done, T + 2)
                            weigh(t, pv_done)
                            pe.wait_ge(khat_done, T + 1)
                            project(T + 2, t + 2)
                            pe.wait_ge(pvs_ready, pair * 2 + (par + 1))
                            select(par)
            ffn_tensor(pe)


_INS = ["x", "ctx_2048", "g_xattn", "g_ffn", "L0_xattn_Wq", "L0_xattn_Wk", "L0_xattn_Wv", "L0_ffn_W_gate",
        "L0_ffn_W_qkv"]


def kernel(**inputs):
    import numpy as _np
    import concourse.bacc as _bacc
    from concourse import mybir as _mybir
    from concourse.bass_utils import run_bass_kernel_spmd as _run

    nc = _bacc.Bacc("TRN2", target_bir_lowering=False, num_devices=1)
    arrays, args = {}, []
    for name in _INS:
        a = _np.ascontiguousarray(inputs[name])
        arrays[f"in_{name}_dram"] = a
        args.append(nc.dram_tensor(f"in_{name}_dram", a.shape, _mybir.dt.from_np(a.dtype), kind="ExternalInput").ap())
    args.append(nc.dram_tensor("out_0_dram", (B, N, D), _mybir.dt.float32, kind="ExternalOutput").ap())
    gated_attention_kernel(nc, *args)
    r = _run(nc, [arrays], core_ids=[0])
    return r.results[0]["out_0_dram"]
```

```python
from contextlib import ExitStack

import concourse.bass as bass
from concourse import mybir

F32 = mybir.dt.float32
F32R = mybir.dt.float32r
F16 = mybir.dt.float16
BF16 = mybir.dt.bfloat16
ALU = mybir.AluOpType
ACT = mybir.ActivationFunctionType
AX = mybir.AxisListType

P = 128
B, N, D = 32, 56, 256
M = 1500
H, DH = 32, 8
FH, FD = 16, 16
TILES = 12
MT = M // TILES
PAIRS = B // 2
HALF = 64
IC = D // P
G = 8
TRI = (H + 2) // 3
VW = DH + 1
PAIR_TILES = 2 * TILES
AHEAD_P, AHEAD_T = 3, 5
VB = 6
LN_EPS, RMS_EPS = 1e-5, 1e-6
MASKED = -3.0e38


def gated_attention_kernel(nc, x, ctx_in, g_xattn, g_ffn, wq, wk, wv, w_gate, w_qkv, out):
    with ExitStack() as stack:
        def sb(name, shape, dt=F32):
            return stack.enter_context(nc.sbuf_tensor(name, shape, dt))

        def psum(name, shape):
            return stack.enter_context(nc.psum_tensor(name, shape, F32))

        def sem(name):
            return stack.enter_context(nc.semaphore(name))

        S = psum("S", [P, 4, 512])
        PV = psum("PV", [P, 512])
        Y = psum("Y", [P, 512])
        XC = psum("XC", [P, 512])
        XK = psum("XK", [P, 512])
        x_ctx = XC[:, 0:256].rearrange("p (c m) -> p c m", c=IC)
        x_key = XK[:, 0:256].bitcast(F16).rearrange("p (c m) -> p c m", c=4)

        ident = sb("ident", [P, P])
        ident16 = sb("ident16", [P, P], F16)
        mask4 = sb("mask4", [P, 4])
        mask_q = sb("mask_q", [P, 4, N], F16)
        mask8 = sb("mask8", [P, 8])
        causal = sb("causal", [HALF, HALF], BF16)
        spread = sb("spread", [HALF, 8, N], BF16)
        gates = sb("gates", [P, 2])
        tg = sb("tg", [P, 2])
        wn_kv = sb("wn_kv", [P, 2, 2, D])
        wn_q = sb("wn_q", [P, 2, D])
        wn_qkv = sb("wn_qkv", [P, 6, D])
        wn_g = sb("wn_g", [FH, D])
        w_hi = sb("w_hi", [P, IC, 2, H, DH], F32R)
        w_lo = sb("w_lo", [P, IC, 2, H, DH], F32R)
        wq_t = sb("wq_t", [P, IC, D])
        wqkv_t = sb("wqkv_t", [P, IC, 3 * D])
        wg_t = sb("wg_t", [P, IC, FH])
        xs = sb("xs", [P, PAIRS, D])
        q_t = sb("q_t", [P, G, PAIRS + 1, P], F16)

        CH = 4
        stats = sb("stats", [P, 2, PAIRS, 6])
        mv = sb("mv", [P, 2, PAIRS, 2])
        ve = sb("ve", [P, 2, PAIRS])
        vln = sb("vln", [P, 2, PAIRS])
        rst = sb("rst", [P, 2, PAIRS])
        nt = sb("nt", [P, CH * H])
        xn = sb("xn", [P, CH, D])
        xn_t = sb("xn_t", [P, CH, IC, P])
        q_sb = sb("q_sb", [P, CH * H, DH])
        q_sq = sb("q_sq", [P, CH * H, DH])
        q_ms = sb("q_ms", [P, CH * H])
        q_ln = sb("q_ln", [P, CH * H])
        q_r = sb("q_r", [P, CH * H])
        q4 = sb("q4", [P, CH, G, 4, 32], F16)

        cx = sb("cx", [P, 2, TILES, D])
        cth = sb("cth", [P, 2, IC, P], F32R)
        ctl = sb("ctl", [P, 2, IC, P], F32R)
        v9 = sb("v9", [P, VB, 33 * VW + 8])
        ksq = sb("ksq", [P, 2, H, DH])
        kms = sb("kms", [P, 2, H])
        kme = sb("kme", [P, 2, H])
        kln = sb("kln", [P, 2, H])
        kr0 = sb("kr0", [P, 2, H])
        kmh = sb("kmh", [P, H])
        kn1 = sb("kn1", [P, H])
        c_eps = sb("c_eps", [P, H])
        c_half = sb("c_half", [P, H])
        c_three = sb("c_three", [P, H])
        kn2 = sb("kn2", [P, H])
        kn3 = sb("kn3", [P, H])
        kr = sb("kr", [P, 2, H])
        kc = sb("kc", [P, 2, H, DH])
        khat = sb("khat", [P, H, DH])
        kp = sb("kp", [P, 2, G, 2, 32], F16)
        kt = sb("kt", [P, G, P], F16)
        q_bd = sb("q_bd", [P, 2, G, 4, N], F16)
        prob = sb("prob", [P, 2, H * N])
        pvs = sb("pvs", [P, 504])
        got = sb("got", [P, H * VW])
        rden = sb("rden", [P, H])
        rdg = sb("rdg", [P, H])
        att = sb("att", [P, H, DH])

        xn2 = sb("xn2", [P, D])
        xt2 = sb("xt2", [P, IC, P])
        qt2 = sb("qt2", [P, 2, P])
        gmax = sb("gmax", [P, 1])
        gdif = sb("gdif", [P, FH])
        gexp = sb("gexp", [P, FH])
        gsum = sb("gsum", [P, 1])
        top1 = sb("top1", [P, 1])
        first = sb("first", [P, FH])
        gkey = sb("gkey", [P, FH])
        gkmax = sb("gkmax", [P, 1])
        pick = sb("pick", [P, FH])
        kvm = sb("kvm", [P, 2, FH, FD])
        kvs = sb("kvs", [P, 2, FD])
        ks_rep = sb("ks_rep", [P, 8, FD])
        ks_t = sb("ks_t", [P, P])
        ks_bd = sb("ks_bd", [P, 2, 8, N])
        vsh = sb("vsh", [P, FD])
        vs_bd = sb("vs_bd", [P, 2, 2, FD + 1])
        smax = sb("smax", [P, FH])
        sdif = sb("sdif", [P, FH, N])
        pr = sb("pr", [P, FH, HALF])
        pt = sb("pt", [P, 8, P])
        ry = sb("ry", [P, FH])
        yo = sb("yo", [P, FH, FD])

        s_mem, s_id, s_const, s_ld, s_wt, s_wc, s_tanh = map(sem, (
            "s_mem", "s_id", "s_const", "s_ld", "s_wt", "s_wc", "s_tanh"))
        s_vz = sem("s_vz")
        s_dc = sem("s_dc")
        ln_stat, ln_agg, ln_ve, ln_ln, ln_r0, ln_x = map(sem, (
            "ln_stat", "ln_agg", "ln_ve", "ln_ln", "ln_r0", "ln_x"))
        nw = sem("nw")
        q_tr, q_te, q_mm, q_cp, q_sqd, q_msd, q_lnd, q_r0, q_hat, q_hi, q_lo, q_t4, q_done = map(sem, (
            "q_tr", "q_te", "q_mm", "q_cp", "q_sqd", "q_msd", "q_lnd", "q_r0", "q_hat", "q_hi", "q_lo", "q_t4",
            "q_done"))
        ctx_loaded = [sem("ctx_loaded0"), sem("ctx_loaded1")]
        t1_done, cth_ready, ctl_ready, proj_done, sq_done, ms_done, me_done, kln_done, r0_done = map(sem, (
            "t1_done", "cth_ready", "ctl_ready", "proj_done", "sq_done", "ms_done", "me_done", "kln_done",
            "r0_done"))
        newton, khat_done, hi_done, lo_done, t2_done, kt_ready = map(sem, (
            "newton", "khat_done", "hi_done", "lo_done", "t2_done", "kt_ready"))
        y_free = sem("y_free")
        sca_done, scb_done, expa_done, expb_done, qbd_ready = map(sem, (
            "sca_done", "scb_done", "expa_done", "expb_done", "qbd_ready"))
        pv_done, pvs_ready, sel_done, pv_free, den_done, rdg_done, x1_done = map(sem, (
            "pv_done", "pvs_ready", "sel_done", "pv_free", "den_done", "rdg_done", "x1_done"))
        att_done = sem("att_done")

        f_xn, f_t1, f_xt, f_proj, f_gate, f_qt = map(sem, (
            "f_xn", "f_t1", "f_xt", "f_proj", "f_gate", "f_qt"))
        f_gdif, f_gexp, f_kv, f_rep, f_t2, f_kst, f_ksb, f_vsb, f_att, f_smax, f_sdif, f_exp = map(sem, (
            "f_gdif", "f_gexp", "f_kv", "f_rep", "f_t2", "f_kst", "f_ksb", "f_vsb", "f_att", "f_smax", "f_sdif",
            "f_exp"))
        f_t3, f_pt, f_y, f_ry, f_out, f_stored = map(sem, ("f_t3", "f_pt", "f_y", "f_ry", "f_out", "f_stored"))

        def ffn_store(sp):
            with sp.Fori(0, PAIRS) as t:
                sp.wait_ge(f_out, t + 1)
                for j in range(2):
                    sp.dma_start(out[bass.ds(t * 2 + j, 1)].rearrange("o n d -> (o n) d"),
                                 xs[HALF * j:HALF * j + N, bass.ds(t, 1)].rearrange("p o d -> p (o d)")
                                 ).then_inc(f_stored, 16)
            sp.wait_ge(f_stored, 16 * B)

        def ffn_gpsimd(pool):
            with pool.Fori(0, PAIRS) as t:
                pool.wait_ge(f_kst, t + 1)
                nc.gpsimd.tensor_tensor(
                    ks_bd[:], ks_t[:].rearrange("p (j o k) -> p j o k", j=2, o=1)[:, :, :, 0:N]
                    .broadcast_to((P, 2, 8, N)),
                    mask8[:].rearrange("p (j h o) -> p j h o", j=1, o=1).broadcast_to((P, 2, 8, N)), ALU.mult
                ).then_inc(f_ksb, 1)

        def norm_estimate(act, which):
            act.wait_ge(ln_ve, which + 1)
            nc.scalar.activation(vln[:, which], ve[:, which], ACT.Ln).then_inc(ln_ln, 1)
            act.wait_ge(ln_ln, which + 1)
            nc.scalar.activation(rst[:, which], vln[:, which], ACT.Exp, scale=-0.5).then_inc(ln_r0, 1)

        def newton_step(dve, y, arg, tmp, base):
            nc.vector.tensor_tensor(tmp, y, y, ALU.mult).then_inc(nw, 1)
            dve.wait_ge(nw, base + 1)
            nc.vector.scalar_tensor_tensor(tmp, tmp, -0.5, arg, ALU.mult, ALU.mult).then_inc(nw, 1)
            dve.wait_ge(nw, base + 2)
            nc.vector.scalar_tensor_tensor(y, tmp, 1.5, y, ALU.add, ALU.mult).then_inc(nw, 1)
            dve.wait_ge(nw, base + 3)

        def layer_norm(dve, which, nw_base):
            for t in range(PAIRS):
                nc.vector.bn_stats(stats[:, which, t], xs[:, t]).then_inc(ln_stat, 1)
            for t in range(PAIRS):
                dve.wait_ge(ln_stat, which * PAIRS + t + 1)
                nc.vector.bn_aggr(mv[:, which, t], stats[:, which, t]).then_inc(ln_agg, 1)
            dve.wait_ge(ln_agg, (which + 1) * PAIRS)
            nc.vector.tensor_scalar(ve[:, which], mv[:, which, :, 1], LN_EPS, None, ALU.add).then_inc(ln_ve, 1)
            dve.wait_ge(ln_r0, which + 1)
            newton_step(dve, rst[:, which], ve[:, which], nt[:, 0:PAIRS], nw_base)

        def normed(dst, which, t):
            tile = bass.ds(t, 1)
            return nc.vector.tensor_scalar(
                dst, xs[:, tile].rearrange("p o d -> p (o d)"), mv[:, which, tile, 0], rst[:, which, tile],
                ALU.subtract, ALU.mult)

        def ffn_scalar(act):
            norm_estimate(act, 1)
            with act.Fori(0, PAIRS) as t:
                act.wait_ge(f_t1, t + 1)
                nc.scalar.copy(xt2[:], x_ctx).then_inc(f_xt, 1)
                act.wait_ge(f_proj, t + 1)
                nc.scalar.copy(qt2[:], XK[:, 0:256].rearrange("p (c m) -> p c m", c=2)).then_inc(f_qt, 1)
                act.wait_ge(f_gdif, t + 1)
                nc.scalar.activation(gexp[:], gdif[:], ACT.Exp).then_inc(f_gexp, 1)
                act.wait_ge(f_t2, t + 1)
                nc.scalar.copy(ks_t[:], XC[:, 256:384]).then_inc(f_kst, 1)
                act.wait_ge(f_sdif, t + 1)
                nc.scalar.activation(pr[:, :, 0:N], sdif[:], ACT.Exp, scale=FD ** -0.5).then_inc(f_exp, 1)
                act.wait_ge(f_t3, t + 1)
                nc.scalar.copy(pt[:].rearrange("p (a h) q -> p a (h q)", a=2), S[:, 2:4]).then_inc(f_pt, 1)

        def ffn_vector(dve):
            dve.wait_ge(x1_done, B)
            layer_norm(dve, 1, 3 + 3 * CH)
            with dve.Fori(0, PAIRS) as t:
                row = xs[:, bass.ds(t, 1)].rearrange("p o d -> p (o d)")
                normed(xn2[:], 1, t).then_inc(f_xn, 1)
                logits = XK[:, 256:256 + FH]
                dve.wait_ge(f_proj, t + 1)
                dve.wait_ge(f_qt, t + 1)
                nc.vector.tensor_reduce(gmax[:], logits, AX.X, ALU.max).then_inc(f_gate, 1)
                dve.wait_ge(f_gate, t * 8 + 1)
                nc.vector.tensor_scalar(gdif[:], logits, gmax[:], None, ALU.subtract).then_inc(f_gdif, 1)
                nc.vector.scalar_tensor_tensor(gkey[:], logits, gmax[:], first[:], ALU.is_equal, ALU.mult
                                               ).then_inc(f_gate, 1)
                dve.wait_ge(f_gate, t * 8 + 2)
                nc.vector.tensor_reduce(gkmax[:], gkey[:], AX.X, ALU.max).then_inc(f_gate, 1)
                dve.wait_ge(f_gate, t * 8 + 3)
                nc.vector.tensor_scalar(pick[:], gkey[:], gkmax[:], None, ALU.is_equal).then_inc(f_gate, 1)
                dve.wait_ge(f_gate, t * 8 + 4)
                nc.vector.tensor_tensor(kvm[:], Y[:].rearrange("p (e h d) -> p e h d", e=2, h=FH),
                                        pick[:].rearrange("p (e h o) -> p e h o", e=1, o=1)
                                        .broadcast_to((P, 2, FH, FD)), ALU.mult).then_inc(f_gate, 1)
                dve.wait_ge(f_gate, t * 8 + 5)
                nc.vector.tensor_reduce(kvs[:], kvm[:].rearrange("p e h d -> p e d h"), AX.X, ALU.add
                                        ).then_inc(f_kv, 1)
                dve.wait_ge(f_kv, t + 1)
                nc.vector.tensor_copy(ks_rep[:], kvs[:, 0:1].broadcast_to((P, 8, FD))).then_inc(f_rep, 1)
                dve.wait_ge(f_gexp, t + 1)
                nc.vector.tensor_reduce(gsum[:], gexp[:], AX.X, ALU.add).then_inc(f_gate, 1)
                dve.wait_ge(f_gate, t * 8 + 6)
                nc.vector.reciprocal(top1[:], gsum[:]).then_inc(f_gate, 1)
                dve.wait_ge(f_gate, t * 8 + 7)
                nc.vector.tensor_scalar(vsh[:], kvs[:, 1], top1[:], None, ALU.mult).then_inc(f_gate, 1)
                dve.wait_ge(f_gate, t * 8 + 8)
                for j in range(2):
                    for h in range(2):
                        tail = nc.vector.tensor_copy(vs_bd[HALF * h:HALF * h + HALF, j, h, 0:FD],
                                                     vsh[HALF * j:HALF * j + HALF])
                tail.then_inc(f_vsb, 1)
                scores = S[:, 0:2, 0:8 * N].rearrange("p c (h k) -> p c h k", h=8)
                dve.wait_ge(f_att, t + 1)
                nc.vector.tensor_reduce(smax[:].rearrange("p (c h) -> p c h", c=2), scores, AX.X, ALU.max
                                        ).then_inc(f_smax, 1)
                dve.wait_ge(f_smax, t + 1)
                nc.vector.tensor_tensor(sdif[:].rearrange("p (c h) k -> p c h k", c=2), scores,
                                        smax[:].rearrange("p (c h o) -> p c h o", c=2, o=1)
                                        .broadcast_to((P, 2, 8, N)), ALU.subtract).then_inc(f_sdif, 1)
                got = PV[:, 0:FH * (FD + 1)].rearrange("p (h c) -> p h c", c=FD + 1)
                dve.wait_ge(f_y, t + 1)
                nc.vector.reciprocal(ry[:], got[:, :, FD]).then_inc(f_ry, 1)
                dve.wait_ge(f_ry, t * 3 + 1)
                nc.vector.tensor_scalar(ry[:], ry[:], tg[:, 1:2], None, ALU.mult).then_inc(f_ry, 1)
                dve.wait_ge(f_ry, t * 3 + 2)
                nc.vector.tensor_tensor(yo[:], got[:, :, 0:FD], ry[:].rearrange("p (h o) -> p h o", o=1)
                                        .broadcast_to((P, FH, FD)), ALU.mult).then_inc(f_ry, 1)
                dve.wait_ge(f_ry, t * 3 + 3)
                nc.vector.tensor_tensor(row, row, yo[:].rearrange("p h d -> p (h d)"), ALU.add).then_inc(f_out, 1)

        def ffn_tensor(pe):
            pe.wait_ge(kt_ready, B * TILES + 1)
            pe.wait_ge(x1_done, B)
            with pe.Fori(0, PAIRS) as t:
                pe.wait_ge(f_xn, t + 1)
                for c in range(IC):
                    tail = nc.tensor.transpose(x_ctx[:, c], xn2[:, c * P:c * P + P], ident[:])
                tail.then_inc(f_t1, 1)
                pe.wait_ge(f_xt, t + 1)
                for c in range(IC):
                    nc.tensor.matmul(XK[:, 256:256 + FH], xt2[:, c], wg_t[:, c], start=(c == 0),
                                     stop=(c == IC - 1))
                for o in range(2):
                    for c in range(IC):
                        nc.tensor.matmul(XK[:, o * P:o * P + P], wqkv_t[:, c, o * P:o * P + P], xt2[:, c],
                                         start=(c == 0), stop=(c == IC - 1))
                for c in range(IC):
                    tail = nc.tensor.matmul(Y[:], xt2[:, c], wqkv_t[:, c, D:3 * D], start=(c == 0),
                                            stop=(c == IC - 1))
                tail.then_inc(f_proj, 1)
                pe.wait_ge(f_rep, t + 1)
                nc.tensor.transpose(XC[:, 256:384], ks_rep[:].rearrange("p h d -> p (h d)"), ident[:]
                                    ).then_inc(f_t2, 1)
                pe.wait_ge(f_qt, t + 1)
                pe.wait_ge(f_ksb, t + 1)
                for c in range(2):
                    for j in range(2):
                        dst = S[HALF * j:HALF * j + HALF, c, 0:8 * N]
                        nc.tensor.matmul(dst, qt2[:, c, HALF * j:HALF * j + HALF],
                                         ks_bd[:, j].rearrange("p h k -> p (h k)"), start=True, stop=False)
                        tail = nc.tensor.matmul(dst, causal[:], spread[:].rearrange("p h k -> p (h k)"),
                                                start=False, stop=True)
                tail.then_inc(f_att, 1)
                pe.wait_ge(f_exp, t + 1)
                for h in range(8):
                    tail = nc.tensor.transpose(S[:, 2 + h // 4, (h % 4) * P:(h % 4 + 1) * P],
                                               pr[:, 2 * h:2 * h + 2].rearrange("p a k -> p (a k)"), ident[:])
                tail.then_inc(f_t3, 1)
                pe.wait_ge(f_pt, t + 1)
                pe.wait_ge(f_vsb, t + 1)
                for h in range(8):
                    for j in range(2):
                        tail = nc.tensor.matmul(
                            PV[HALF * j:HALF * j + HALF, h * 2 * (FD + 1):(h + 1) * 2 * (FD + 1)],
                            pt[:, h, HALF * j:HALF * j + HALF], vs_bd[:, j].rearrange("p h d -> p (h d)"),
                            start=True, stop=True)
                tail.then_inc(f_y, 1)

        block = stack.enter_context(nc.Block())
        N_LOADS = 9

        @block.sync
        def _(sp):
            sp.wait_ge(s_mem, 1)
            for j in range(2):
                sp.dma_start(xs[HALF * j:HALF * j + N], x.rearrange("(p j) n d -> j n p d", j=2)[j]).then_inc(s_ld, 16)
            sp.dma_start(wn_q[:], wq.rearrange("(r p) i -> p r i", p=P)).then_inc(s_ld, 16)
            sp.dma_start(wn_kv[:, 0], wk.rearrange("(r p) i -> p r i", p=P)).then_inc(s_ld, 16)
            sp.dma_start(wn_kv[:, 1], wv.rearrange("(r p) i -> p r i", p=P)).then_inc(s_ld, 16)
            sp.dma_start(wn_qkv[:], w_qkv.rearrange("(r p) i -> p r i", p=P)).then_inc(s_ld, 16)
            sp.dma_start(wn_g[:], w_gate).then_inc(s_ld, 16)
            sp.dma_start(gates[:, 0:1], g_xattn.rearrange("(o a) -> o a", o=1).broadcast_to((P, 1))).then_inc(s_ld, 16)
            sp.dma_start(gates[:, 1:2], g_ffn.rearrange("(o a) -> o a", o=1).broadcast_to((P, 1))).then_inc(s_ld, 16)
            rows = ctx_in.rearrange("b (p t) d -> b p t d", t=TILES)
            for b in range(2):
                sp.dma_start(cx[0:MT, b], rows[b]).then_inc(ctx_loaded[b], 16)
            with sp.Fori(0, PAIRS - 1) as pair:
                for b in range(2):
                    sp.wait_ge(t1_done, pair * PAIR_TILES + TILES * (b + 1))
                    sp.dma_start(cx[0:MT, b], rows[bass.ds(pair * 2 + (2 + b), 1)].rearrange("o p t d -> (o p) t d")
                                 ).then_inc(ctx_loaded[b], 16)
            sp.wait_ge(t1_done, B * TILES - TILES)
            sp.dma_start(cx[0:MT, 0], rows[0]).then_inc(ctx_loaded[0], 16)
            ffn_store(sp)

        @block.gpsimd
        def _(pool):
            nc.gpsimd.memset(c_eps[:], RMS_EPS)
            nc.gpsimd.memset(c_half[:], -0.5)
            nc.gpsimd.memset(c_three[:], 1.5)
            nc.gpsimd.memset(ident[:], 0.0).then_inc(s_id, 1)
            pool.wait_ge(s_id, 1)
            nc.gpsimd.affine_select(out=ident[:], in_=ident[:], compare_op=ALU.not_equal, fill=1.0, base=0,
                                    pattern=[[-1, P]], channel_multiplier=1).then_inc(s_id, 1)
            nc.gpsimd.memset(causal[:], 0.0).then_inc(s_id, 1)
            pool.wait_ge(s_id, 3)
            nc.gpsimd.affine_select(out=causal[:], in_=causal[:], compare_op=ALU.is_ge, fill=MASKED, base=0,
                                    pattern=[[1, HALF]], channel_multiplier=-1).then_inc(s_id, 1)

            def build_q(par, pair):
                src = q_t[:, :, bass.ds(pair, 1), HALF * par:HALF * par + N]
                nc.gpsimd.tensor_tensor(
                    q_bd[:, par], src.rearrange("p g o n -> p g o n").broadcast_to((P, G, 4, N)),
                    mask_q[:].rearrange("p (o h) n -> p o h n", o=1).broadcast_to((P, G, 4, N)),
                    ALU.mult).then_inc(qbd_ready, 1)

            def keys_rsqrt(T, k):
                pool.wait_ge(ms_done, T + 1)
                nc.gpsimd.tensor_tensor(kme[:, k % 2], kms[:, k % 2], c_eps[:], ALU.add).then_inc(me_done, 1)
                pool.wait_ge(me_done, T + 1)
                pool.wait_ge(r0_done, T + 1)
                nc.gpsimd.tensor_tensor(kmh[:], kme[:, k % 2], c_half[:], ALU.mult)
                nc.gpsimd.tensor_tensor(kn1[:], kr0[:, k % 2], kr0[:, k % 2], ALU.mult).then_inc(newton, 1)
                pool.wait_ge(newton, T * 4 + 1)
                nc.gpsimd.tensor_tensor(kn2[:], kn1[:], kmh[:], ALU.mult).then_inc(newton, 1)
                pool.wait_ge(newton, T * 4 + 2)
                nc.gpsimd.tensor_tensor(kn3[:], kn2[:], c_three[:], ALU.add).then_inc(newton, 1)
                pool.wait_ge(newton, T * 4 + 3)
                nc.gpsimd.tensor_tensor(kr[:, k % 2], kn3[:], kr0[:, k % 2], ALU.mult).then_inc(newton, 1)

            pool.wait_ge(s_const, 1)
            pool.wait_ge(q_done, CH)
            build_q(0, 0)
            for k in range(AHEAD_P + 1):
                keys_rsqrt(k, k)
            with pool.Fori(0, PAIRS) as pair:
                T0 = pool.snap(pair * PAIR_TILES)
                for k in range(1, PAIR_TILES + 1):
                    keys_rsqrt(T0 + (k + AHEAD_P), k + AHEAD_P)
                    if k % TILES == 2:
                        par = k // TILES
                        build_q(1 - par, pair + par)
            ffn_gpsimd(pool)

        @block.scalar
        def _(act):
            act.wait_ge(s_ld, 16 * N_LOADS)
            nc.scalar.activation(tg[:], gates[:], ACT.Tanh).then_inc(s_tanh, 1)
            nc.scalar.preload_act_table_set("natural_log_exp_and_others")
            act.wait_ge(s_wt, 1)
            nc.scalar.copy(wq_t[:].rearrange("p c (r o) -> p c r o", r=2),
                           S[:, 2].rearrange("p (c r o) -> p c r o", c=IC, r=2)).then_inc(s_wc, 1)
            for n, bank in enumerate((S[:, 3], Y, XK)):
                nc.scalar.copy(wqkv_t[:, :, n * 256:n * 256 + 256].rearrange("p c (r o) -> p c r o", r=2),
                               bank[:].rearrange("p (c r o) -> p c r o", c=IC, r=2)).then_inc(s_wc, 1)
            nc.scalar.copy(wg_t[:], XC[:, 0:IC * FH].rearrange("p (c o) -> p c o", c=IC)).then_inc(s_wc, 1)

            norm_estimate(act, 0)
            with act.Fori(0, CH) as c:
                act.wait_ge(q_tr, c + 1)
                nc.scalar.copy(xn_t[:].rearrange("p (a u) c m -> p a (u c m)", a=2), S[:, 0:2]).then_inc(q_te, 1)
                act.wait_ge(q_mm, c + 1)
                nc.scalar.activation(q_sq[:].rearrange("p (a h) d -> p a (h d)", a=2), S[:, 2:4], ACT.Square,
                                     scale=DH ** -0.5).then_inc(q_sqd, 1)
                nc.scalar.copy(q_sb[:].rearrange("p (a h) d -> p a (h d)", a=2), S[:, 2:4]).then_inc(q_cp, 1)
                act.wait_ge(q_msd, c + 1)
                nc.scalar.activation(q_ln[:], q_ms[:], ACT.Ln).then_inc(q_lnd, 1)
                act.wait_ge(q_lnd, c + 1)
                nc.scalar.activation(q_r[:], q_ln[:], ACT.Exp, scale=-0.5).then_inc(q_r0, 1)

            def drain_projection(T, k):
                act.wait_ge(proj_done, T + 1)
                nc.scalar.copy(v9[:, k % VB, 0:H * VW].rearrange("p (h c) -> p h c", c=VW)[:, :, 0:DH],
                               Y[:, 256:512].rearrange("p (h d) -> p h d", d=DH))
                y_keys = Y[:, 0:256].rearrange("p (h d) -> p h d", d=DH)
                nc.scalar.activation(ksq[:, k % 2], y_keys, ACT.Square, scale=DH ** -0.5).then_inc(sq_done, 1)
                if k >= 2:
                    act.wait_ge(khat_done, T - 1)
                nc.scalar.copy(kc[:, k % 2], y_keys).then_inc(y_free, 1)

            def context_hi(T, k):
                act.wait_ge(t1_done, T + 1)
                nc.scalar.copy(cth[:, k % 2], x_ctx).then_inc(cth_ready, 1)

            def keys_estimate(T, k):
                act.wait_ge(me_done, T + 1)
                nc.scalar.activation(kln[:, k % 2], kme[:, k % 2], ACT.Ln).then_inc(kln_done, 1)
                act.wait_ge(kln_done, T + 1)
                nc.scalar.activation(kr0[:, k % 2], kln[:, k % 2], ACT.Exp, scale=-0.5).then_inc(r0_done, 1)

            def exps(T, k, half, scores, done):
                act.wait_ge(scores, T + 1)
                dst = prob[0:MT, k % 2, half * 896:half * 896 + 896].rearrange("p (a n) -> p a n", a=2)
                nc.scalar.activation(dst, S[0:MT, 2 * half:2 * half + 2, 0:448], ACT.Exp,
                                     scale=DH ** -0.5).then_inc(done, 1)

            act.wait_ge(q_cp, CH)
            nc.scalar.copy(kln[:, 0], q_ln[:, 0:H]).then_inc(expa_done, 1)
            nc.scalar.copy(kln[:, 1], q_ln[:, 0:H]).then_inc(expb_done, 1)
            context_hi(0, 0)
            for k in range(AHEAD_P):
                context_hi(k + 1, k + 1)
                drain_projection(k, k)
                keys_estimate(k, k)
            context_hi(4, 4)

            def act_step(T, k, pair):
                drain_projection(T + 3, k + 3)
                if k and k % TILES == 0:
                    act.wait_ge(pv_done, pair * 2 + k // TILES)
                    nc.scalar.copy(pvs[:], PV[:, 0:504]).then_inc(pvs_ready, 1)
                exps(T, k, 0, sca_done, expa_done)
                context_hi(T + 5, k + 5)
                exps(T, k, 1, scb_done, expb_done)
                keys_estimate(T + 3, k + 3)
                if k and k % TILES == 0:
                    rows = slice(HALF * (k // TILES - 1), HALF * (k // TILES - 1) + N)
                    act.wait_ge(sel_done, pair * 2 + k // TILES)
                    nc.scalar.copy(got[rows], PV[rows, 0:H * VW]).then_inc(pv_free, 1)

            act_step(0, 0, 0)
            with act.Fori(0, PAIRS) as pair:
                T0 = act.snap(pair * PAIR_TILES)
                for k in range(1, PAIR_TILES + 1):
                    act_step(T0 + k, k, pair)
            ffn_scalar(act)

        @block.vector
        def _(dve):
            nc.vector.memset(xs[:], 0.0)
            nc.vector.memset(cx[96:P], 0.0).then_inc(s_mem, 1)
            nc.vector.memset(v9[:], 1.0)
            nc.vector.memset(q_t[:, :, PAIRS], 0.0)
            nc.vector.memset(pr[:], 0.0)
            nc.vector.memset(vs_bd[:], 0.0).then_inc(s_vz, 1)
            dve.wait_ge(s_vz, 1)
            for h in range(2):
                nc.vector.memset(vs_bd[HALF * h:HALF * h + HALF, :, h, FD], 1.0)
            for h in range(FH):
                nc.vector.memset(first[:, h:h + 1], float(FH - h))
            dve.wait_ge(s_id, 4)
            nc.vector.tensor_copy(ident16[:], ident[:])
            nc.vector.tensor_reduce(mask4[:], ident[:].rearrange("p (q h d) -> p h q d", q=4, h=4), AX.XY,
                                    ALU.add).then_inc(s_dc, 1)
            nc.vector.tensor_reduce(mask8[:], ident[:].rearrange("p (h d) -> p h d", h=8), AX.X, ALU.add)
            nc.vector.tensor_copy(spread[:], ident[0:HALF, 0:N].rearrange("p (o k) -> p o k", o=1)
                                  .broadcast_to((HALF, 8, N)))
            dve.wait_ge(s_dc, 1)
            nc.vector.tensor_copy(mask_q[:], mask4[:].rearrange("p (h o) -> p h o", o=1).broadcast_to((P, 4, N))
                                  ).then_inc(s_const, 1)

            dve.wait_ge(s_wt, 1)
            for w in range(2):
                for c in range(IC):
                    for r in range(2):
                        src = S[:, w].rearrange("p (c r h d e) -> p c r e h d", c=IC, r=2, h=8, d=DH)[:, c, r]
                        at = w * 16 + r * 8
                        nc.vector.tensor_copy(w_hi[:, c, :, at:at + 8], src).then_inc(s_dc, 1)
            dve.wait_ge(s_dc, 9)
            for w in range(2):
                for c in range(IC):
                    for r in range(2):
                        src = S[:, w].rearrange("p (c r h d e) -> p c r e h d", c=IC, r=2, h=8, d=DH)[:, c, r]
                        at = w * 16 + r * 8
                        nc.vector.tensor_tensor(w_lo[:, c, :, at:at + 8], src,
                                                w_hi[:, c, :, at:at + 8].bitcast(F32), ALU.subtract
                                                ).then_inc(s_wc, 1)

            dve.wait_ge(s_ld, 16 * N_LOADS)
            layer_norm(dve, 0, 0)
            with dve.Fori(0, CH) as c:
                for u in range(CH):
                    normed(xn[:, u], 0, c * CH + u).then_inc(ln_x, 1)
                dve.wait_ge(q_sqd, c + 1)
                nc.vector.tensor_reduce(q_ms[:], q_sq[:], AX.X, ALU.add).then_inc(q_hat, 1)
                dve.wait_ge(q_hat, c * 3 + 1)
                nc.vector.tensor_scalar(q_ms[:], q_ms[:], RMS_EPS, None, ALU.add).then_inc(q_msd, 1)
                dve.wait_ge(q_r0, c + 1)
                newton_step(dve, q_r[:], q_ms[:], nt[:], c * 3 + 3)
                dve.wait_ge(q_cp, c + 1)
                nc.vector.tensor_tensor(q_sb[:], q_sb[:], q_r[:].rearrange("p (h o) -> p h o", o=1)
                                        .broadcast_to((P, CH * H, DH)), ALU.mult).then_inc(q_hat, 1)
                dve.wait_ge(q_hat, c * 3 + 2)
                hat = q_sb[:].rearrange("p (g o h) d -> p g o (h d)", o=1, h=4).broadcast_to((P, CH * G, 2, 32))
                q4v = q4[:].rearrange("p u g a r -> p (u g) a r")
                nc.vector.tensor_copy(q4v[:, :, 0:2], hat).then_inc(q_hat, 1)
                dve.wait_ge(q_hat, c * 3 + 3)
                nc.vector.tensor_tensor(q4v[:, :, 2:4], hat, q4v[:, :, 0:2], ALU.subtract).then_inc(q_lo, 1)
                dve.wait_ge(q_t4, c + 1)
                for u, bank in enumerate((XC, Y, XK, PV)):
                    tail = nc.vector.tensor_copy(q_t[:, :, bass.ds(c * CH + u, 1)].rearrange("p g o m -> p g (o m)"),
                                                 bank[:].bitcast(F16).rearrange("p (g m) -> p g m", g=G))
                tail.then_inc(q_done, 1)

            def context_lo(T, k):
                dve.wait_ge(cth_ready, T + 1)
                nc.vector.tensor_tensor(ctl[:, k % 2], x_ctx, cth[:, k % 2].bitcast(F32), ALU.subtract
                                        ).then_inc(ctl_ready, 1)

            def keys_ms(T, k):
                dve.wait_ge(sq_done, T + 1)
                nc.vector.tensor_reduce(kms[:, k % 2], ksq[:, k % 2], AX.X, ALU.add).then_inc(ms_done, 1)

            def keys_norm(T, k):
                dve.wait_ge(newton, T * 4 + 4)
                nc.vector.tensor_tensor(khat[:], kc[:, k % 2],
                                        kr[:, k % 2].rearrange("p (h o) -> p h o", o=1).broadcast_to((P, H, DH)),
                                        ALU.mult).then_inc(khat_done, 1)

            hat = khat[:].rearrange("p (g h) d -> p g (h d)", h=4)

            def keys_hi(T, k):
                dve.wait_ge(khat_done, T + 1)
                nc.vector.tensor_copy(kp[:, k % 2, :, 0], hat).then_inc(hi_done, 1)

            def keys_lo(T, k):
                dve.wait_ge(hi_done, T + 1)
                nc.vector.tensor_tensor(kp[:, k % 2, :, 1], hat, kp[:, k % 2, :, 0], ALU.subtract
                                        ).then_inc(lo_done, 1)

            def keys_spread(T, k):
                dve.wait_ge(t2_done, T + 1)
                for odd in range(2):
                    for dst in range(2):
                        tail = nc.vector.tensor_copy(
                            kt[HALF * dst:HALF * dst + HALF].rearrange("p (c o) m -> p c o m", o=2)[:, :, odd],
                            x_key[HALF * odd:HALF * odd + HALF])
                tail.then_inc(kt_ready, 1)

            def normalise(par, pair):
                rows = slice(HALF * par, HALF * par + N)
                sums = got[rows].rearrange("p (h c) -> p h c", c=VW)
                n = pair * 2 + (par + 1)
                dve.wait_ge(pv_free, n + 1)
                nc.vector.reciprocal(rden[rows], sums[:, :, DH]).then_inc(den_done, 1)
                dve.wait_ge(den_done, n)
                nc.vector.tensor_scalar(rdg[rows], rden[rows], tg[rows, 0:1], None, ALU.mult).then_inc(rdg_done, 1)
                dve.wait_ge(rdg_done, n)
                nc.vector.tensor_tensor(att[rows], sums[:, :, 0:DH], rdg[rows].rearrange("p (h o) -> p h o", o=1)
                                        .broadcast_to((N, H, DH)), ALU.mult).then_inc(att_done, 1)
                dve.wait_ge(att_done, n)
                row = xs[rows, bass.ds(pair, 1)].rearrange("p o d -> p (o d)")
                nc.vector.tensor_tensor(row, row, att[rows].rearrange("p h d -> p (h d)"), ALU.add
                                        ).then_inc(x1_done, 1)

            def dve_step(T, k, pair):
                keys_ms(T + 3, k + 3)
                keys_spread(T + 1, k + 1)
                keys_norm(T + 2, k + 2)
                context_lo(T + 5, k + 5)
                keys_hi(T + 2, k + 2)
                keys_lo(T + 2, k + 2)
                if k and k % TILES == 0:
                    normalise(k // TILES - 1, pair)

            dve.wait_ge(q_done, CH)
            nc.vector.memset(PV[:], 1.0).then_inc(pv_free, 1)
            dve.wait_ge(s_tanh, 1)
            context_lo(0, 0)
            context_lo(1, 1)
            for k in range(AHEAD_P):
                keys_ms(k, k)
                context_lo(k + 2, k + 2)
                if k < 2:
                    keys_norm(k, k)
                    keys_hi(k, k)
                    keys_lo(k, k)
            keys_spread(0, 0)
            dve_step(0, 0, 0)
            with dve.Fori(0, PAIRS) as pair:
                T0 = dve.snap(pair * PAIR_TILES)
                for k in range(1, PAIR_TILES + 1):
                    dve_step(T0 + k, k, pair)
            ffn_vector(dve)

        @block.tensor
        def _(pe):
            pe.wait_ge(s_id, 4)
            pe.wait_ge(s_ld, 16 * N_LOADS)
            for w in range(2):
                for c in range(IC):
                    for r in range(2):
                        nc.tensor.transpose(S[:, w, (c * 2 + r) * P:(c * 2 + r + 1) * P],
                                            wn_kv[:, w, r, c * P:c * P + P], ident[:])
            for c in range(IC):
                for r in range(2):
                    nc.tensor.transpose(S[:, 2, (c * 2 + r) * P:(c * 2 + r + 1) * P], wn_q[:, r, c * P:c * P + P],
                                        ident[:])
            for n, bank in enumerate((S[:, 3], Y, XK)):
                for c in range(IC):
                    for r in range(2):
                        nc.tensor.transpose(bank[:, (c * 2 + r) * P:(c * 2 + r + 1) * P],
                                            wn_qkv[:, 2 * n + r, c * P:c * P + P], ident[:])
            for c in range(IC):
                tail = nc.tensor.transpose(XC[:, c * FH:c * FH + FH], wn_g[:, c * P:c * P + P], ident[0:FH, 0:FH])
            tail.then_inc(s_wt, 1)
            pe.wait_ge(s_wc, 13)

            with pe.Fori(0, CH) as c:
                pe.wait_ge(ln_x, c * CH + CH)
                for u in range(CH):
                    for k in range(IC):
                        tail = nc.tensor.transpose(S[:, u // 2, ((u % 2) * IC + k) * P:((u % 2) * IC + k + 1) * P],
                                                   xn[:, u, k * P:k * P + P], ident[:])
                tail.then_inc(q_tr, 1)
                pe.wait_ge(q_te, c + 1)
                for u in range(CH):
                    for k in range(IC):
                        tail = nc.tensor.matmul(S[:, 2 + u // 2, (u % 2) * D:(u % 2) * D + D], xn_t[:, u, k],
                                                wq_t[:, k], start=(k == 0), stop=(k == IC - 1))
                tail.then_inc(q_mm, 1)
                pe.wait_ge(q_lo, c + 1)
                for u, bank in enumerate((XC, Y, XK, PV)):
                    for g in range(G):
                        tail = nc.tensor.transpose(bank[:].bitcast(F16)[:, g * P:g * P + P],
                                                   q4[:, u, g].rearrange("p a r -> p (a r)"), ident16[:])
                tail.then_inc(q_t4, 1)
                pe.wait_ge(q_done, c + 1)

            def context_transpose(T, k):
                tile = k % TILES
                for c in range(IC):
                    tail = nc.tensor.transpose(x_ctx[:, c], cx[:, (k // TILES) % 2, tile, c * P:c * P + P], ident[:])
                tail.then_inc(t1_done, 1)

            def project(k):
                steps = [(a, w, c) for a, w in ((cth, w_hi), (cth, w_lo), (ctl, w_hi)) for c in range(IC)]
                for n, (a, w, c) in enumerate(steps):
                    tail = nc.tensor.matmul(Y[:], a[:, k % 2, c], w[:, c].rearrange("p e h d -> p (e h d)"),
                                            start=(n == 0), stop=(n == len(steps) - 1))
                tail.then_inc(proj_done, 1)

            def key_transpose(T, k):
                for c in range(4):
                    tail = nc.tensor.transpose(x_key[:, c], kp[:, k % 2, 2 * c:2 * c + 2].rearrange(
                        "p g a r -> p (g a r)"), ident16[:])
                tail.then_inc(t2_done, 1)

            def score(par, half, done):
                for g in range(4 * half, 4 * half + 4):
                    tail = nc.tensor.matmul(S[:, g // 2, (g % 2) * 4 * N:(g % 2 + 1) * 4 * N], kt[:, g],
                                            q_bd[:, par, g].rearrange("p h n -> p (h n)"), start=True, stop=True)
                tail.then_inc(done, 1)

            def weigh(k):
                tile = k % TILES
                for j in range(TRI):
                    quad, slot = j % 4, j // 4
                    n = min(3 * N, H * N - 3 * N * j)
                    tail = nc.tensor.matmul(PV[32 * quad:32 * quad + 32, slot * 3 * N:slot * 3 * N + n],
                                            v9[0:MT, k % VB, j * 3 * VW:j * 3 * VW + 32],
                                            prob[0:MT, k % 2, j * 3 * N:j * 3 * N + n],
                                            start=(tile == 0 and slot == 0), stop=(tile == TILES - 1),
                                            skip_group_check=True)
                if tile == TILES - 1:
                    tail.then_inc(pv_done, 1)

            def select(par):
                for slot in range(3):
                    for a in range(3):
                        dst = PV[HALF * par:HALF * par + N, 0:36 * VW].rearrange("p (s i a c) -> p s a i c", s=3, i=4,
                                                                                a=3)[:, slot, a]
                        tail = nc.tensor.matmul(
                            dst, pvs[:, slot * 3 * N + a * N:slot * 3 * N + a * N + N],
                            ident[:].rearrange("p (i r) -> p i r", r=32)[:, :, a * VW:a * VW + VW],
                            start=True, stop=True)
                tail.then_inc(sel_done, 1)

            pe.wait_ge(ctx_loaded[0], 16)
            context_transpose(0, 0)
            for k in range(AHEAD_P):
                pe.wait_ge(ctl_ready, k + 1)
                context_transpose(k + 1, k + 1)
                if k > 0:
                    pe.wait_ge(y_free, k)
                project(k)
            pe.wait_ge(ctl_ready, 4)
            context_transpose(4, 4)
            pe.wait_ge(lo_done, 1)
            key_transpose(0, 0)

            def pe_step(T, k, pair):
                par = (k // TILES) % 2
                ends = k > 0 and k % TILES == 0
                pe.wait_ge(y_free, T + 3)
                project(k + 3)
                if ends:
                    pe.wait_ge(expb_done, T + 1)
                    weigh(k - 1)
                if k % TILES == 0:
                    pe.wait_ge(qbd_ready, pair * 2 + (k // TILES + 1))
                pe.wait_ge(kt_ready, T + 1)
                pe.wait_ge(expa_done, T + 1)
                score(par, 0, sca_done)
                pe.wait_ge(expb_done, T + 1)
                score(par, 1, scb_done)
                if (k + AHEAD_T) % TILES == 0:
                    pe.wait_ge(ctx_loaded[1 - par], (pair + (1 + par)) * 16)
                pe.wait_ge(ctl_ready, T + 5)
                context_transpose(T + 5, k + 5)
                if ends:
                    pe.wait_ge(pvs_ready, pair * 2 + k // TILES)
                    select(k // TILES - 1)
                pe.wait_ge(lo_done, T + 2)
                key_transpose(T + 1, k + 1)
                if k % TILES == 1:
                    pe.wait_ge(pv_free, pair * 2 + (k // TILES + 1))
                if k > 0 and not ends:
                    weigh(k - 1)

            pe_step(0, 0, 0)
            with pe.Fori(0, PAIRS) as pair:
                T0 = pe.snap(pair * PAIR_TILES)
                for k in range(1, PAIR_TILES + 1):
                    pe_step(T0 + k, k, pair)
            ffn_tensor(pe)


_INS = ["x", "ctx_2048", "g_xattn", "g_ffn", "L0_xattn_Wq", "L0_xattn_Wk", "L0_xattn_Wv", "L0_ffn_W_gate",
        "L0_ffn_W_qkv"]


def kernel(**inputs):
    import numpy as _np
    import concourse.bacc as _bacc
    from concourse import mybir as _mybir
    from concourse.bass_utils import run_bass_kernel_spmd as _run

    nc = _bacc.Bacc("TRN2", target_bir_lowering=False, num_devices=1)
    arrays, args = {}, []
    for name in _INS:
        a = _np.ascontiguousarray(inputs[name])
        arrays[f"in_{name}_dram"] = a
        args.append(nc.dram_tensor(f"in_{name}_dram", a.shape, _mybir.dt.from_np(a.dtype), kind="ExternalInput").ap())
    args.append(nc.dram_tensor("out_0_dram", (B, N, D), _mybir.dt.float32, kind="ExternalOutput").ap())
    gated_attention_kernel(nc, *args)
    r = _run(nc, [arrays], core_ids=[0])
    return r.results[0]["out_0_dram"]
```

```python
from contextlib import ExitStack

import concourse.bass as bass
from concourse import mybir

F32 = mybir.dt.float32
F32R = mybir.dt.float32r
F16 = mybir.dt.float16
BF16 = mybir.dt.bfloat16
ALU = mybir.AluOpType
ACT = mybir.ActivationFunctionType
AX = mybir.AxisListType

P = 128
B, N, D = 32, 56, 256
M = 1500
H, DH = 32, 8
FH, FD = 16, 16
TILES = 12
MT = M // TILES
PAIRS = B // 2
HALF = 64
IC = D // P
G = 8
HQ = H // 4
SLOTS = ((0, 3), (3, 3), (6, 2))
VW = DH + 1
PAIR_TILES = 2 * TILES
CT = 2
CHUNKS = PAIRS // CT
AHEAD_P, AHEAD_T = 3, 5
SEL_W = 4 * VW
SEL_XC = (HQ - 1) * SEL_W
VB = 6
LN_EPS, RMS_EPS = 1e-5, 1e-6
MASKED = -3.0e38


def gated_attention_kernel(nc, x, ctx_in, g_xattn, g_ffn, wq, wk, wv, w_gate, w_qkv, out):
    with ExitStack() as stack:
        def sb(name, shape, dt=F32):
            return stack.enter_context(nc.sbuf_tensor(name, shape, dt))

        def psum(name, shape):
            return stack.enter_context(nc.psum_tensor(name, shape, F32))

        def sem(name):
            return stack.enter_context(nc.semaphore(name))

        S = psum("S", [P, 4, 512])
        PV = psum("PV", [P, 512])
        Y = psum("Y", [P, 512])
        XC = psum("XC", [P, 512])
        XK = psum("XK", [P, 512])
        x_ctx = XC[:, 0:256].rearrange("p (c m) -> p c m", c=IC)
        x_key = XK[:, 0:256].bitcast(F16).rearrange("p (c m) -> p c m", c=4)

        ident = sb("ident", [P, P])
        ident16 = sb("ident16", [P, P], F16)
        mask4 = sb("mask4", [P, 4])
        mask_q = sb("mask_q", [P, 4, N], F16)
        mask8 = sb("mask8", [P, 8])
        causal = sb("causal", [HALF, HALF], BF16)
        spread = sb("spread", [HALF, 8, N], BF16)
        gates = sb("gates", [P, 2])
        tg = sb("tg", [P, 2])
        wn_kv = sb("wn_kv", [P, 2, 2, D])
        wn_q = sb("wn_q", [P, 2, D])
        wn_qkv = sb("wn_qkv", [P, 6, D])
        wn_g = sb("wn_g", [FH, D])
        w_hi = sb("w_hi", [P, IC, 2, H, DH], F32R)
        w_lo = sb("w_lo", [P, IC, 2, H, DH], F32R)
        wq_t = sb("wq_t", [P, IC, D])
        wqkv_t = sb("wqkv_t", [P, IC, 3 * D])
        wg_t = sb("wg_t", [P, IC, FH])
        xs = sb("xs", [P, PAIRS + 1, D])
        q_t = sb("q_t", [P, G, PAIRS + 1, P], F16)

        stats = sb("stats", [P, 2, PAIRS + 1, 6])
        mv = sb("mv", [P, 2, PAIRS, 2])
        ve = sb("ve", [P, 2, PAIRS])
        vln = sb("vln", [P, 2, PAIRS])
        rst = sb("rst", [P, 2, PAIRS])
        nt = sb("nt", [P, CT * H])
        xn = sb("xn", [P, 2, CT, D])
        xn_t = sb("xn_t", [P, 2, CT, IC, P])
        q_sb = sb("q_sb", [P, 2, CT * H, DH])
        q_ms = sb("q_ms", [P, CT * H])
        q_ln = sb("q_ln", [P, CT * H])
        q_r = sb("q_r", [P, CT * H])
        q4 = sb("q4", [P, 2, CT * G, 4, 32], F16)

        cx = sb("cx", [P, 2, TILES, D])
        cth = sb("cth", [P, 2, IC, P], F32R)
        ctl = sb("ctl", [P, 2, IC, P], F32R)
        v9 = sb("v9", [P, VB, H * VW])
        ksq = sb("ksq", [P, 2, H, DH])
        kms = sb("kms", [P, 2, H])
        kme = sb("kme", [P, 2, H])
        kln = sb("kln", [P, 2, H])
        kr0 = sb("kr0", [P, 2, H])
        kmh = sb("kmh", [P, H])
        kn1 = sb("kn1", [P, H])
        c_eps = sb("c_eps", [P, H])
        c_half = sb("c_half", [P, H])
        c_three = sb("c_three", [P, H])
        kn2 = sb("kn2", [P, H])
        kn3 = sb("kn3", [P, H])
        kr = sb("kr", [P, 2, H])
        kc = sb("kc", [P, 2, H, DH])
        khat = sb("khat", [P, H, DH])
        kp = sb("kp", [P, 2, G, 2, 32], F16)
        kt = sb("kt", [P, G, P], F16)
        q_bd = sb("q_bd", [P, 2, G, 4, N], F16)
        prob = sb("prob", [P, 2, H * N])
        q_sq = prob[:, 0, 0:2 * CT * H * DH].rearrange("p (b h d) -> p b h d", b=2, d=DH)
        pvs = sb("pvs", [P, HQ * N])
        got = sb("got", [P, H * VW])
        rden = sb("rden", [P, H])
        att = sb("att", [P, H, DH])

        xn2 = sb("xn2", [P, D])
        xt2 = sb("xt2", [P, IC, P])
        qt2 = sb("qt2", [P, 2, 2, P])
        gmax = sb("gmax", [P, 1])
        gdif = sb("gdif", [P, FH])
        gexp = sb("gexp", [P, FH])
        gsum = sb("gsum", [P, 1])
        top1 = sb("top1", [P, 1])
        first = sb("first", [P, FH])
        gkey = sb("gkey", [P, FH])
        gkmax = sb("gkmax", [P, 1])
        pick = sb("pick", [P, FH])
        kvm = sb("kvm", [P, 2, FH, FD])
        kvs = sb("kvs", [P, 2, FD])
        ks_rep = sb("ks_rep", [P, 8, FD])
        ks_t = sb("ks_t", [P, P])
        ks_bd = sb("ks_bd", [P, 2, 8, N])
        vsh = sb("vsh", [P, 2, FD])
        vs_bd = sb("vs_bd", [P, 2, 2, 2, FD + 1])
        smax = sb("smax", [P, FH])
        sdif = sb("sdif", [P, FH, N])
        pr = sb("pr", [P, FH, HALF])
        pt = sb("pt", [P, 8, P])
        ry = sb("ry", [P, FH])
        yo = sb("yo", [P, FH, FD])

        ld_q, ld_kv, ld_qkv, ld_gates, ld_pad = map(sem, (
            "ld_q", "ld_kv", "ld_qkv", "ld_gates", "ld_pad"))
        ld_x = [sem("ld_x0"), sem("ld_x1")]
        wt_q, wt_kv, wt_qkv, wc_act, wc_kv = map(sem, ("wt_q", "wt_kv", "wt_qkv", "wc_act", "wc_kv"))
        s_fill, s_id, s_const, s_tanh = map(sem, ("s_fill", "s_id", "s_const", "s_tanh"))
        s_dc = sem("s_dc")
        ln_stat, ln_agg, ln_ve, ln_ln, ln_r0, ln_x = map(sem, (
            "ln_stat", "ln_agg", "ln_ve", "ln_ln", "ln_r0", "ln_x"))
        nw = sem("nw")
        q_tr, q_te, q_mm, q_cp, q_sqd, q_msd, q_lnd, q_r0, q_red, q_hat, q_hi, q_lo1, q_lo, q_t4, q_done = map(sem, (
            "q_tr", "q_te", "q_mm", "q_cp", "q_sqd", "q_msd", "q_lnd", "q_r0", "q_red", "q_hat", "q_hi", "q_lo1",
            "q_lo", "q_t4", "q_done"))
        ctx_loaded = [sem("ctx_loaded0"), sem("ctx_loaded1")]
        t1_done, cth_ready, ctl_ready, proj_done, sq_done, ms_done, me_done, kln_done, r0_done = map(sem, (
            "t1_done", "cth_ready", "ctl_ready", "proj_done", "sq_done", "ms_done", "me_done", "kln_done",
            "r0_done"))
        newton, khat_done, hi_done, lo_done, t2_done, kt_ready = map(sem, (
            "newton", "khat_done", "hi_done", "lo_done", "t2_done", "kt_ready"))
        y_free = sem("y_free")
        sca_done, scb_done, expa_done, expb_done, qbd_ready = map(sem, (
            "sca_done", "scb_done", "expa_done", "expb_done", "qbd_ready"))
        pv_done, pvs_ready, sel_done, got_done, den_done, x1_done = map(sem, (
            "pv_done", "pvs_ready", "sel_done", "got_done", "den_done", "x1_done"))
        att_done = sem("att_done")

        f_xn, f_t1, f_xt, f_q, f_proj, f_gate, f_qt, f_vs = map(sem, (
            "f_xn", "f_t1", "f_xt", "f_q", "f_proj", "f_gate", "f_qt", "f_vs"))
        f_gdif, f_gexp, f_kv, f_rep, f_t2, f_kst, f_ksb, f_vsb, f_att, f_smax, f_sdif, f_exp = map(sem, (
            "f_gdif", "f_gexp", "f_kv", "f_rep", "f_t2", "f_kst", "f_ksb", "f_vsb", "f_att", "f_smax", "f_sdif",
            "f_exp"))
        f_t3, f_pt, f_y, f_ry, f_out, f_stored = map(sem, ("f_t3", "f_pt", "f_y", "f_ry", "f_out", "f_stored"))

        def q_steps(eng, step, after_first=None):
            for c in range(3):
                step(c, c)
                if c == 0 and after_first:
                    after_first()
            with eng.Fori(0, (CHUNKS - 4) // 2) as i:
                C = eng.snap(i * 2)
                for c in (3, 4):
                    step(c, C + c)
            for c in range(CHUNKS - 1, CHUNKS + 2):
                step(c, c)

        def is_chunk(c):
            return 0 <= c < CHUNKS

        def ffn_steps(eng, step):
            for u in range(-4, 2):
                step(u, u)
            with eng.Fori(0, (PAIRS - 6) // 2) as i:
                U = eng.snap(i * 2)
                for u in (2, 3):
                    step(u, U + u)
            for u in range(PAIRS - 4, PAIRS):
                step(u, u)

        def is_tile(t):
            return 0 <= t < PAIRS

        def ffn_store(sp):
            with sp.Fori(0, PAIRS) as t:
                sp.wait_ge(f_out, t + 1)
                for j in range(2):
                    sp.dma_start(out[bass.ds(t * 2 + j, 1)].rearrange("o n d -> (o n) d"),
                                 xs[HALF * j:HALF * j + N, bass.ds(t + 1, 1)].rearrange("p o d -> p (o d)")
                                 ).then_inc(f_stored, 16)
            sp.wait_ge(f_stored, 16 * B)

        def ffn_gpsimd(pool):
            def build_k(T):
                pool.wait_ge(f_kst, T + 1)
                nc.gpsimd.tensor_tensor(
                    ks_bd[:], ks_t[:].rearrange("p (j o k) -> p j o k", j=2, o=1)[:, :, :, 0:N]
                    .broadcast_to((P, 2, 8, N)),
                    mask8[:].rearrange("p (j h o) -> p j h o", j=1, o=1).broadcast_to((P, 2, 8, N)), ALU.mult
                ).then_inc(f_ksb, 1)

            with pool.Fori(0, PAIRS) as t:
                build_k(t)

        NORMS = ((0, 0, PAIRS // 2), (0, PAIRS // 2, PAIRS), (1, 0, PAIRS - 1), (1, PAIRS - 1, PAIRS))

        def norm_estimate(act, n):
            which, first_tile, end = NORMS[n]
            tiles = slice(first_tile, end)
            act.wait_ge(ln_ve, n + 1)
            nc.scalar.activation(vln[:, which, tiles], ve[:, which, tiles], ACT.Ln).then_inc(ln_ln, 1)
            act.wait_ge(ln_ln, n + 1)
            nc.scalar.activation(rst[:, which, tiles], vln[:, which, tiles], ACT.Exp, scale=-0.5).then_inc(ln_r0, 1)

        def newton_step(dve, y, arg, tmp, base):
            nc.vector.tensor_tensor(tmp, y, y, ALU.mult).then_inc(nw, 1)
            dve.wait_ge(nw, base + 1)
            nc.vector.scalar_tensor_tensor(tmp, tmp, -0.5, arg, ALU.mult, ALU.mult).then_inc(nw, 1)
            dve.wait_ge(nw, base + 2)
            nc.vector.scalar_tensor_tensor(y, tmp, 1.5, y, ALU.add, ALU.mult).then_inc(nw, 1)
            dve.wait_ge(nw, base + 3)

        def norm_variance(dve, n):
            which, first_tile, end = NORMS[n]
            for t in range(first_tile, end):
                dve.wait_ge(ln_stat, which * (PAIRS + 1) + t + 1)
                nc.vector.bn_aggr(mv[:, which, t], stats[:, which, t + 1]).then_inc(ln_agg, 1)
            dve.wait_ge(ln_agg, which * PAIRS + end)
            nc.vector.tensor_scalar(ve[:, which, first_tile:end], mv[:, which, first_tile:end, 1], LN_EPS, None, ALU.add
                                    ).then_inc(ln_ve, 1)

        def norm_root(dve, n, nw_base):
            which, first_tile, end = NORMS[n]
            dve.wait_ge(ln_r0, n + 1)
            newton_step(dve, rst[:, which, first_tile:end], ve[:, which, first_tile:end], nt[:, 0:end - first_tile],
                        nw_base)

        def normed(dst, which, t):
            tile = bass.ds(t, 1)
            return nc.vector.tensor_scalar(
                dst, xs[:, bass.ds(t + 1, 1)].rearrange("p o d -> p (o d)"), mv[:, which, tile, 0], rst[:, which, tile],
                ALU.subtract, ALU.mult)

        def ffn_scalar(act):
            def gate_exp(T):
                act.wait_ge(f_gdif, T + 1)
                nc.scalar.activation(gexp[:], gdif[:], ACT.Exp, accum_out=gsum[:]).then_inc(f_gexp, 1)

            def x_out(T):
                act.wait_ge(f_t1, T + 1)
                nc.scalar.copy(xt2[:], x_ctx).then_inc(f_xt, 1)

            def probs_out(T):
                act.wait_ge(f_t3, T + 1)
                nc.scalar.copy(pt[:].rearrange("p (a h) q -> p a (h q)", a=2), S[:, 2:4]).then_inc(f_pt, 1)

            def values(t, T):
                act.wait_ge(f_vs, T + 1)
                for j in range(2):
                    for h in range(2):
                        tail = nc.scalar.copy(vs_bd[HALF * h:HALF * h + HALF, t % 2, j, h, 0:FD],
                                              vsh[HALF * j:HALF * j + HALF, t % 2])
                tail.then_inc(f_vsb, 1)

            def k_out(t, T):
                act.wait_ge(f_t2, T + 1)
                if t > 0:
                    act.wait_ge(f_ksb, T)
                nc.scalar.copy(ks_t[:], XC[:, 256:384]).then_inc(f_kst, 1)

            def score_exp(T):
                act.wait_ge(f_sdif, T + 1)
                nc.scalar.activation(pr[:, :, 0:N], sdif[:], ACT.Exp, scale=FD ** -0.5).then_inc(f_exp, 1)

            def q_out(t, T):
                act.wait_ge(f_q, T + 1)
                nc.scalar.copy(qt2[:, t % 2], XK[:, 0:256].rearrange("p (c m) -> p c m", c=2)).then_inc(f_qt, 1)

            def step(u, U):
                if u == -2:
                    norm_estimate(act, 3)
                if is_tile(u + 3):
                    x_out(U + 3)
                if is_tile(u):
                    probs_out(U)
                if is_tile(u + 2):
                    k_out(u + 2, U + 2)
                if is_tile(u + 1):
                    values(u + 1, U + 1)
                if is_tile(u + 3):
                    q_out(u + 3, U + 3)
                if is_tile(u + 1):
                    score_exp(U + 1)
                if is_tile(u + 3):
                    gate_exp(U + 3)

            ffn_steps(act, step)

        def ffn_vector(dve):

            def row(T):
                return xs[:, bass.ds(T + 1, 1)].rearrange("p o d -> p (o d)")

            def gate(t, T):
                logits = XK[:, 256:256 + FH]
                dve.wait_ge(f_q, T + 1)
                dve.wait_ge(f_qt, T + 1)
                nc.vector.tensor_reduce(gmax[:], logits, AX.X, ALU.max).then_inc(f_gate, 1)
                dve.wait_ge(f_gate, T * 6 + 1)
                nc.vector.tensor_scalar(gdif[:], logits, gmax[:], None, ALU.subtract).then_inc(f_gdif, 1)
                nc.vector.scalar_tensor_tensor(gkey[:], logits, gmax[:], first[:], ALU.is_equal, ALU.mult
                                               ).then_inc(f_gate, 1)
                dve.wait_ge(f_gate, T * 6 + 2)
                nc.vector.tensor_reduce(gkmax[:], gkey[:], AX.X, ALU.max).then_inc(f_gate, 1)
                dve.wait_ge(f_gate, T * 6 + 3)
                nc.vector.tensor_scalar(pick[:], gkey[:], gkmax[:], None, ALU.is_equal).then_inc(f_gate, 1)
                dve.wait_ge(f_gate, T * 6 + 4)
                dve.wait_ge(f_proj, T + 1)
                nc.vector.tensor_tensor(kvm[:], Y[:].rearrange("p (e h d) -> p e h d", e=2, h=FH),
                                        pick[:].rearrange("p (e h o) -> p e h o", e=1, o=1)
                                        .broadcast_to((P, 2, FH, FD)), ALU.mult).then_inc(f_gate, 1)
                dve.wait_ge(f_gate, T * 6 + 5)
                nc.vector.tensor_reduce(kvs[:], kvm[:].rearrange("p e h d -> p e d h"), AX.X, ALU.add
                                        ).then_inc(f_kv, 1)
                dve.wait_ge(f_kv, T + 1)
                nc.vector.tensor_copy(ks_rep[:], kvs[:, 0:1].broadcast_to((P, 8, FD))).then_inc(f_rep, 1)
                dve.wait_ge(f_gexp, T + 1)
                nc.vector.reciprocal(top1[:], gsum[:]).then_inc(f_gate, 1)
                dve.wait_ge(f_gate, T * 6 + 6)
                if t >= 2:
                    dve.wait_ge(f_vsb, T - 1)
                nc.vector.tensor_scalar(vsh[:, t % 2], kvs[:, 1], top1[:], tg[:, 1:2], ALU.mult, ALU.mult
                                        ).then_inc(f_vs, 1)

            def centre(t, T):
                scores = S[:, 0:2, 0:8 * N].rearrange("p c (h k) -> p c h k", h=8)
                dve.wait_ge(f_att, T + 1)
                nc.vector.tensor_reduce(smax[:].rearrange("p (c h) -> p c h", c=2), scores, AX.X, ALU.max
                                        ).then_inc(f_smax, 1)
                dve.wait_ge(f_smax, T + 1)
                if t > 0:
                    dve.wait_ge(f_exp, T)
                nc.vector.tensor_tensor(sdif[:].rearrange("p (c h) k -> p c h k", c=2), scores,
                                        smax[:].rearrange("p (c h o) -> p c h o", c=2, o=1)
                                        .broadcast_to((P, 2, 8, N)), ALU.subtract).then_inc(f_sdif, 1)

            def finish(T):
                got = PV[:, 0:FH * (FD + 1)].rearrange("p (h c) -> p h c", c=FD + 1)
                dve.wait_ge(f_y, T + 1)
                nc.vector.reciprocal(ry[:], got[:, :, FD]).then_inc(f_ry, 1)
                dve.wait_ge(f_ry, T * 2 + 1)
                nc.vector.tensor_tensor(yo[:], got[:, :, 0:FD], ry[:].rearrange("p (h o) -> p h o", o=1)
                                        .broadcast_to((P, FH, FD)), ALU.mult).then_inc(f_ry, 1)
                dve.wait_ge(f_ry, T * 2 + 2)
                nc.vector.tensor_tensor(row(T), row(T), yo[:].rearrange("p h d -> p (h d)"), ALU.add
                                        ).then_inc(f_out, 1)

            def step(u, U):
                if is_tile(u + 1):
                    centre(u + 1, U + 1)
                if is_tile(u + 4) and u + 4 > 0:
                    dve.wait_ge(f_t1, U + 4)
                    normed(xn2[:], 1, U + 4).then_inc(f_xn, 1)
                if is_tile(u + 3):
                    gate(u + 3, U + 3)
                if is_tile(u):
                    finish(U)
                if u == -2:
                    norm_root(dve, 3, 9 + 3 * CHUNKS)

            ffn_steps(dve, step)

        def ffn_tensor(pe):
            pe.wait_ge(got_done, B + 1)

            def x_transpose(T):
                pe.wait_ge(f_xn, T + 1)
                for c in range(IC):
                    tail = nc.tensor.transpose(x_ctx[:, c], xn2[:, c * P:c * P + P], ident[:])
                tail.then_inc(f_t1, 1)

            def project2(t, T):
                pe.wait_ge(f_xt, T + 1)
                if t > 0:
                    pe.wait_ge(f_rep, T)
                for c in range(IC):
                    nc.tensor.matmul(XK[:, 256:256 + FH], xt2[:, c], wg_t[:, c], start=(c == 0),
                                     stop=(c == IC - 1))
                for o in range(2):
                    for c in range(IC):
                        tail = nc.tensor.matmul(XK[:, o * P:o * P + P], wqkv_t[:, c, o * P:o * P + P], xt2[:, c],
                                                start=(c == 0), stop=(c == IC - 1))
                tail.then_inc(f_q, 1)
                for c in range(IC):
                    tail = nc.tensor.matmul(Y[:], xt2[:, c], wqkv_t[:, c, D:3 * D], start=(c == 0),
                                            stop=(c == IC - 1))
                tail.then_inc(f_proj, 1)

            def k_transpose(t, T):
                pe.wait_ge(f_rep, T + 1)
                if t + 1 < PAIRS:
                    pe.wait_ge(f_xt, T + 2)
                nc.tensor.transpose(XC[:, 256:384], ks_rep[:].rearrange("p h d -> p (h d)"), ident[:]
                                    ).then_inc(f_t2, 1)

            def score2(t, T):
                pe.wait_ge(f_qt, T + 1)
                pe.wait_ge(f_ksb, T + 1)
                if t > 0:
                    pe.wait_ge(f_sdif, T)
                for c in range(2):
                    for mask in range(2):
                        for j in range(2):
                            dst = S[HALF * j:HALF * j + HALF, c, 0:8 * N]
                            if mask:
                                tail = nc.tensor.matmul(dst, causal[:], spread[:].rearrange("p h k -> p (h k)"),
                                                        start=False, stop=True)
                            else:
                                nc.tensor.matmul(dst, qt2[:, t % 2, c, HALF * j:HALF * j + HALF],
                                                 ks_bd[:, j].rearrange("p h k -> p (h k)"), start=True, stop=False)
                tail.then_inc(f_att, 1)

            def prob_transpose(t, T):
                pe.wait_ge(f_exp, T + 1)
                for h in range(8):
                    tail = nc.tensor.transpose(S[:, 2 + h // 4, (h % 4) * P:(h % 4 + 1) * P],
                                               pr[:, 2 * h:2 * h + 2].rearrange("p a k -> p (a k)"), ident[:])
                tail.then_inc(f_t3, 1)

            def weigh2(t, T):
                pe.wait_ge(f_pt, T + 1)
                pe.wait_ge(f_vsb, T + 1)
                if t > 0:
                    pe.wait_ge(f_out, T)
                for h in range(8):
                    for j in range(2):
                        tail = nc.tensor.matmul(
                            PV[HALF * j:HALF * j + HALF, h * 2 * (FD + 1):(h + 1) * 2 * (FD + 1)],
                            pt[:, h, HALF * j:HALF * j + HALF], vs_bd[:, t % 2, j].rearrange("p h d -> p (h d)"),
                            start=True, stop=True)
                tail.then_inc(f_y, 1)

            def step(u, U):
                if is_tile(u + 1):
                    score2(u + 1, U + 1)
                if is_tile(u + 3):
                    x_transpose(U + 3)
                if is_tile(u):
                    prob_transpose(u, U)
                if is_tile(u + 2):
                    k_transpose(u + 2, U + 2)
                if is_tile(u + 3):
                    project2(u + 3, U + 3)
                if is_tile(u):
                    weigh2(u, U)

            ffn_steps(pe, step)

        def part_banks(c):
            return (XC, Y) if c % 2 == 0 else (XK, PV)

        def batch_rows(par):
            return slice(HALF * par, HALF * par + N)

        block = stack.enter_context(nc.Block())

        @block.sync
        def _(sp):
            batches = x.rearrange("(p j) n d -> j n p d", j=2)
            for part in range(2):
                at = slice(part * PAIRS // 2, (part + 1) * PAIRS // 2)
                to = slice(at.start + 1, at.stop + 1)
                for j in range(2):
                    sp.dma_start(xs[HALF * j:HALF * j + N, to], batches[j, :, at]).then_inc(ld_x[part], 16)
                    sp.dma_start(xs[HALF * j + N:HALF * j + HALF, to], batches[j, 0:HALF - N, at]
                                 ).then_inc(ld_x[part], 16)
                if part == 0:
                    sp.dma_start(wn_q[:], wq.rearrange("(r p) i -> p r i", p=P)).then_inc(ld_q, 16)
                    sp.dma_start(wn_g[:], w_gate).then_inc(ld_q, 16)
                    for n, g in enumerate((g_xattn, g_ffn)):
                        sp.dma_start(gates[:, n:n + 1], g.rearrange("(o a) -> o a", o=1).broadcast_to((P, 1))
                                     ).then_inc(ld_gates, 16)
            sp.dma_start(wn_kv[:, 0], wk.rearrange("(r p) i -> p r i", p=P)).then_inc(ld_kv, 16)
            sp.dma_start(wn_kv[:, 1], wv.rearrange("(r p) i -> p r i", p=P)).then_inc(ld_kv, 16)
            sp.dma_start(wn_qkv[:], w_qkv.rearrange("(r p) i -> p r i", p=P)).then_inc(ld_qkv, 16)
            rows = ctx_in.rearrange("b (p t) d -> b p t d", t=TILES)
            for b in range(2):
                sp.dma_start(cx[MT:P, b], rows[b, 0:P - MT]).then_inc(ld_pad, 16)
                sp.dma_start(cx[0:MT, b], rows[b]).then_inc(ctx_loaded[b], 16)
            with sp.Fori(0, PAIRS - 1) as pair:
                for b in range(2):
                    sp.wait_ge(t1_done, pair * PAIR_TILES + TILES * (b + 1))
                    sp.dma_start(cx[0:MT, b], rows[bass.ds(pair * 2 + (2 + b), 1)].rearrange("o p t d -> (o p) t d")
                                 ).then_inc(ctx_loaded[b], 16)
            sp.wait_ge(t1_done, B * TILES - TILES)
            sp.dma_start(cx[0:MT, 0], rows[0]).then_inc(ctx_loaded[0], 16)
            ffn_store(sp)

        @block.gpsimd
        def _(pool):
            nc.gpsimd.memset(c_eps[:], RMS_EPS)
            nc.gpsimd.memset(c_half[:], -0.5)
            nc.gpsimd.memset(c_three[:], 1.5)
            nc.gpsimd.memset(ident[:], 0.0).then_inc(s_id, 1)
            pool.wait_ge(s_id, 1)
            nc.gpsimd.affine_select(out=ident[:], in_=ident[:], compare_op=ALU.not_equal, fill=1.0, base=0,
                                    pattern=[[-1, P]], channel_multiplier=1).then_inc(s_id, 1)
            nc.gpsimd.memset(causal[:], 0.0).then_inc(s_id, 1)
            pool.wait_ge(s_id, 3)
            nc.gpsimd.affine_select(out=causal[:], in_=causal[:], compare_op=ALU.is_ge, fill=MASKED, base=0,
                                    pattern=[[1, HALF]], channel_multiplier=-1).then_inc(s_id, 1)

            nc.gpsimd.memset(v9[:], 1.0)
            nc.gpsimd.memset(xs[:, 0], 0.0)
            nc.gpsimd.memset(q_t[:, :, PAIRS], 0.0)
            nc.gpsimd.memset(pr[:], 0.0)
            nc.gpsimd.memset(vs_bd[:], 0.0).then_inc(s_fill, 1)
            pool.wait_ge(s_fill, 1)
            for h in range(2):
                tail = nc.gpsimd.memset(vs_bd[HALF * h:HALF * h + HALF, :, :, h, FD], 1.0)
            tail.then_inc(s_fill, 1)

            def build_q(par, pair, g):
                src = q_t[:, g, bass.ds(pair, 1), HALF * par:HALF * par + N]
                nc.gpsimd.tensor_tensor(q_bd[:, par, g], src.broadcast_to((P, 4, N)), mask_q[:], ALU.mult
                                        ).then_inc(qbd_ready, 1)

            def keys_rsqrt(T, k):
                pool.wait_ge(ms_done, T + 1)
                nc.gpsimd.tensor_tensor(kme[:, k % 2], kms[:, k % 2], c_eps[:], ALU.add).then_inc(me_done, 1)
                pool.wait_ge(me_done, T + 1)
                pool.wait_ge(r0_done, T + 1)
                nc.gpsimd.tensor_tensor(kmh[:], kme[:, k % 2], c_half[:], ALU.mult)
                nc.gpsimd.tensor_tensor(kn1[:], kr0[:, k % 2], kr0[:, k % 2], ALU.mult).then_inc(newton, 1)
                pool.wait_ge(newton, T * 4 + 1)
                nc.gpsimd.tensor_tensor(kn2[:], kn1[:], kmh[:], ALU.mult).then_inc(newton, 1)
                pool.wait_ge(newton, T * 4 + 2)
                nc.gpsimd.tensor_tensor(kn3[:], kn2[:], c_three[:], ALU.add).then_inc(newton, 1)
                pool.wait_ge(newton, T * 4 + 3)
                nc.gpsimd.tensor_tensor(kr[:, k % 2], kn3[:], kr0[:, k % 2], ALU.mult).then_inc(newton, 1)

            pool.wait_ge(s_fill, 2)
            pool.wait_ge(s_const, 1)
            pool.wait_ge(q_done, 1)
            for g in range(G):
                build_q(0, 0, g)
            for k in range(AHEAD_P + 1):
                keys_rsqrt(k, k)
            with pool.Fori(0, PAIRS) as pair:
                T0 = pool.snap(pair * PAIR_TILES)
                for k in range(1, PAIR_TILES + 1):
                    keys_rsqrt(T0 + (k + AHEAD_P), k + AHEAD_P)
                    if 2 <= k % TILES < 2 + G:
                        par = k // TILES
                        build_q(1 - par, pair + par, k % TILES - 2)
            ffn_gpsimd(pool)

        @block.scalar
        def _(act):
            act.wait_ge(ld_gates, 32)
            nc.scalar.activation(tg[:], gates[:], ACT.Tanh).then_inc(s_tanh, 1)
            nc.scalar.preload_act_table_set("natural_log_exp_and_others")

            def weights_out(dst, bank):
                nc.scalar.copy(dst.rearrange("p c (r o) -> p c r o", r=2),
                               bank.rearrange("p (c r o) -> p c r o", c=IC, r=2)).then_inc(wc_act, 1)

            act.wait_ge(wt_q, 1)
            weights_out(wq_t[:], S[:, 3])
            nc.scalar.copy(wg_t[:], S[:, 2, 0:IC * FH].rearrange("p (c o) -> p c o", c=IC)).then_inc(wc_act, 1)
            norm_estimate(act, 0)
            def context_hi(T, k):
                act.wait_ge(t1_done, T + 1)
                nc.scalar.copy(cth[:, k % 2], x_ctx).then_inc(cth_ready, 1)

            def step(c, C):
                if is_chunk(c - 1):
                    act.wait_ge(q_msd, C)
                    nc.scalar.activation(q_ln[:], q_ms[:], ACT.Ln).then_inc(q_lnd, 1)
                    act.wait_ge(q_lnd, C)
                    nc.scalar.activation(q_r[:], q_ln[:], ACT.Exp, scale=-0.5).then_inc(q_r0, 1)
                if is_chunk(c):
                    act.wait_ge(q_tr, C + 1)
                    nc.scalar.copy(xn_t[:, c % 2].rearrange("p u c m -> p (u c m)"), S[:, c % 2]).then_inc(q_te, 1)
                if is_chunk(c - 2):
                    act.wait_ge(q_t4, C - 1)
                    for u in range(CT):
                        tail = nc.scalar.copy(
                            q_t[:, :, bass.ds((C - 2) * CT + u, 1)].rearrange("p g o m -> p g (o m)"),
                            part_banks(c)[u][:].bitcast(F16).rearrange("p (g m) -> p g m", g=G))
                    tail.then_inc(q_done, 1)
                if c == CHUNKS:
                    context_hi(0, 0)
                if is_chunk(c):
                    act.wait_ge(q_mm, C + 1)
                    if c >= 2:
                        act.wait_ge(q_red, C - 1)
                    q = S[:, 2 + c % 2].rearrange("p (h d) -> p h d", d=DH)
                    nc.scalar.activation(q_sq[:, c % 2], q, ACT.Square, scale=DH ** -0.5).then_inc(q_sqd, 1)
                    nc.scalar.copy(q_sb[:, c % 2], q).then_inc(q_cp, 1)

            def after_first():
                norm_estimate(act, 1)
                act.wait_ge(wt_qkv, 1)
                for n, bank in enumerate((S[:, 1], XC[:], Y[:])):
                    weights_out(wqkv_t[:, :, n * 256:n * 256 + 256], bank)

            q_steps(act, step, after_first)

            def drain_projection(T, k):
                act.wait_ge(proj_done, T + 1)
                nc.scalar.copy(v9[:, k % VB, 0:H * VW].rearrange("p (h c) -> p h c", c=VW)[:, :, 0:DH],
                               Y[:, 256:512].rearrange("p (h d) -> p h d", d=DH))
                y_keys = Y[:, 0:256].rearrange("p (h d) -> p h d", d=DH)
                nc.scalar.activation(ksq[:, k % 2], y_keys, ACT.Square, scale=DH ** -0.5).then_inc(sq_done, 1)
                if k >= 2:
                    act.wait_ge(khat_done, T - 1)
                nc.scalar.copy(kc[:, k % 2], y_keys).then_inc(y_free, 1)

            def keys_estimate(T, k):
                act.wait_ge(me_done, T + 1)
                nc.scalar.activation(kln[:, k % 2], kme[:, k % 2], ACT.Ln).then_inc(kln_done, 1)
                act.wait_ge(kln_done, T + 1)
                nc.scalar.activation(kr0[:, k % 2], kln[:, k % 2], ACT.Exp, scale=-0.5).then_inc(r0_done, 1)

            def exps(T, k, half, scores, done):
                act.wait_ge(scores, T + 1)
                dst = prob[0:MT, k % 2, half * 896:half * 896 + 896].rearrange("p (a n) -> p a n", a=2)
                nc.scalar.activation(dst, S[0:MT, 2 * half:2 * half + 2, 0:448], ACT.Exp,
                                     scale=DH ** -0.5).then_inc(done, 1)

            act.wait_ge(s_fill, 2)
            nc.scalar.copy(kln[:, 0], q_ln[:, 0:H]).then_inc(expa_done, 1)
            nc.scalar.copy(kln[:, 1], q_ln[:, 0:H]).then_inc(expb_done, 1)
            context_hi(1, 1)
            for k in range(AHEAD_P):
                drain_projection(k, k)
                context_hi(k + 2, k + 2)
                keys_estimate(k, k)

            def weighted_out(done):
                act.wait_ge(pv_done, done)
                nc.scalar.copy(pvs[:], PV[:, 0:HQ * N]).then_inc(pvs_ready, 1)

            def act_step(T, k, pair):
                if k % TILES == 1:
                    weighted_out(pair * 2 + (k // TILES + 1))
                drain_projection(T + 3, k + 3)
                exps(T, k, 0, sca_done, expa_done)
                if k % TILES == 1:
                    act.wait_ge(t1_done, T + 6)
                    rows = batch_rows(1 - k // TILES)
                    nc.scalar.copy(got[rows, 0:SEL_XC], XC[rows, 256:256 + SEL_XC])
                context_hi(T + 5, k + 5)
                exps(T, k, 1, scb_done, expb_done)
                keys_estimate(T + 3, k + 3)

            act_step(0, 0, 0)
            with act.Fori(0, PAIRS) as pair:
                T0 = act.snap(pair * PAIR_TILES)
                for k in range(1, PAIR_TILES + 1):
                    act_step(T0 + k, k, pair)
            weighted_out(B + 1)
            norm_estimate(act, 2)
            ffn_scalar(act)

        @block.vector
        def _(dve):
            for h in range(FH):
                nc.vector.memset(first[:, h:h + 1], float(FH - h))
            dve.wait_ge(s_id, 4)
            nc.vector.tensor_copy(ident16[:], ident[:])
            nc.vector.tensor_reduce(mask4[:], ident[:].rearrange("p (q h d) -> p h q d", q=4, h=4), AX.XY,
                                    ALU.add).then_inc(s_dc, 1)
            nc.vector.tensor_reduce(mask8[:], ident[:].rearrange("p (h d) -> p h d", h=8), AX.X, ALU.add)
            nc.vector.tensor_copy(spread[:], ident[0:HALF, 0:N].rearrange("p (o k) -> p o k", o=1)
                                  .broadcast_to((HALF, 8, N)))
            dve.wait_ge(s_dc, 1)
            nc.vector.tensor_copy(mask_q[:], mask4[:].rearrange("p (h o) -> p h o", o=1).broadcast_to((P, 4, N))
                                  ).then_inc(s_const, 1)

            def token_stats(part):
                dve.wait_ge(ld_x[part], 64)
                for t in range(part * PAIRS // 2, (part + 1) * PAIRS // 2):
                    nc.vector.bn_stats(stats[:, 0, t + 1], xs[:, t + 1]).then_inc(ln_stat, 1)
                norm_variance(dve, part)

            token_stats(0)
            norm_root(dve, 0, 0)

            def rows_normed(c, C):
                if c >= 2:
                    dve.wait_ge(q_tr, C - 1)
                for u in range(CT):
                    tail = normed(xn[:, c % 2, u], 0, C * CT + u)
                tail.then_inc(ln_x, 1)

            rows_normed(0, 0)
            token_stats(1)
            dve.wait_ge(wt_kv, 1)
            for part in range(2):
                if part:
                    dve.wait_ge(s_dc, 9)
                for w, bank in enumerate((XK, PV)):
                    for c in range(IC):
                        for r in range(2):
                            src = bank[:].rearrange("p (c r h d e) -> p c r e h d", c=IC, r=2, h=8, d=DH)[:, c, r]
                            at = w * 16 + r * 8
                            hi, lo = w_hi[:, c, :, at:at + 8], w_lo[:, c, :, at:at + 8]
                            if part == 0:
                                nc.vector.tensor_copy(hi, src).then_inc(s_dc, 1)
                            else:
                                nc.vector.tensor_tensor(lo, src, hi.bitcast(F32), ALU.subtract).then_inc(wc_kv, 1)

            def step(c, C):
                if is_chunk(c - 1):
                    dve.wait_ge(q_sqd, C)
                    nc.vector.tensor_reduce(q_ms[:], q_sq[:, (c - 1) % 2], AX.X, ALU.add).then_inc(q_red, 1)
                    dve.wait_ge(q_red, C)
                    nc.vector.tensor_scalar(q_ms[:], q_ms[:], RMS_EPS, None, ALU.add).then_inc(q_msd, 1)
                if is_chunk(c + 1):
                    rows_normed(c + 1, C + 1)
                if is_chunk(c - 1):
                    dve.wait_ge(q_r0, C)
                    newton_step(dve, q_r[:], q_ms[:], nt[:], C * 3 if c == 1 else C * 3 + 3)
                    dve.wait_ge(q_cp, C)
                    q = q_sb[:, (c - 1) % 2]
                    nc.vector.tensor_tensor(q, q, q_r[:].rearrange("p (h o) -> p h o", o=1)
                                            .broadcast_to((P, CT * H, DH)), ALU.mult).then_inc(q_hat, 1)
                    dve.wait_ge(q_hat, C)
                    if c >= 3:
                        dve.wait_ge(q_t4, C - 2)
                    hat = q.rearrange("p (g o h) d -> p g o (h d)", o=1, h=4)
                    parts = q4[:, (c - 1) % 2]
                    nc.vector.tensor_copy(parts[:, :, 0:2], hat.broadcast_to((P, CT * G, 2, 32))).then_inc(q_hi, 1)
                    dve.wait_ge(q_hi, C)
                    nc.vector.tensor_tensor(parts[:, :, 2:3], hat, parts[:, :, 0:1], ALU.subtract).then_inc(q_lo1, 1)
                    dve.wait_ge(q_lo1, C)
                    nc.vector.tensor_copy(parts[:, :, 3], parts[:, :, 2]).then_inc(q_lo, 1)
                if c == 1:
                    norm_root(dve, 1, 6)

            q_steps(dve, step)

            def context_lo(T, k):
                dve.wait_ge(cth_ready, T + 1)
                nc.vector.tensor_tensor(ctl[:, k % 2], x_ctx, cth[:, k % 2].bitcast(F32), ALU.subtract
                                        ).then_inc(ctl_ready, 1)

            def keys_ms(T, k):
                dve.wait_ge(sq_done, T + 1)
                nc.vector.tensor_reduce(kms[:, k % 2], ksq[:, k % 2], AX.X, ALU.add).then_inc(ms_done, 1)

            def keys_norm(T, k):
                dve.wait_ge(newton, T * 4 + 4)
                nc.vector.tensor_tensor(khat[:], kc[:, k % 2],
                                        kr[:, k % 2].rearrange("p (h o) -> p h o", o=1).broadcast_to((P, H, DH)),
                                        ALU.mult).then_inc(khat_done, 1)

            hat = khat[:].rearrange("p (g h) d -> p g (h d)", h=4)

            def keys_hi(T, k):
                dve.wait_ge(khat_done, T + 1)
                nc.vector.tensor_copy(kp[:, k % 2, :, 0], hat).then_inc(hi_done, 1)

            def keys_lo(T, k):
                dve.wait_ge(hi_done, T + 1)
                nc.vector.tensor_tensor(kp[:, k % 2, :, 1], hat, kp[:, k % 2, :, 0], ALU.subtract
                                        ).then_inc(lo_done, 1)

            def keys_spread(T, k):
                dve.wait_ge(t2_done, T + 1)
                for odd in range(2):
                    for dst in range(2):
                        tail = nc.vector.tensor_copy(
                            kt[HALF * dst:HALF * dst + HALF].rearrange("p (c o) m -> p c o m", o=2)[:, :, odd],
                            x_key[HALF * odd:HALF * odd + HALF])
                tail.then_inc(kt_ready, 1)

            sums = got[:].rearrange("p (h c) -> p h c", c=VW)

            def end_columns(par, done):
                rows = batch_rows(par)
                nc.vector.tensor_copy(got[rows, SEL_XC:H * VW], XK[rows, 256:256 + H * VW - SEL_XC]
                                      ).then_inc(got_done, 1)

            def end_reciprocal(par, done):
                rows = batch_rows(par)
                dve.wait_ge(got_done, done)
                nc.vector.reciprocal(rden[rows], sums[rows, :, DH]).then_inc(den_done, 1)

            def end_weighted(par, done):
                rows = batch_rows(par)
                dve.wait_ge(den_done, done)
                nc.vector.scalar_tensor_tensor(
                    att[rows], sums[rows, :, 0:DH], tg[rows, 0:1], rden[rows].rearrange("p (h o) -> p h o", o=1)
                    .broadcast_to((N, H, DH)), ALU.mult, ALU.mult).then_inc(att_done, 1)

            def end_add(par, tile, done):
                rows = batch_rows(par)
                dve.wait_ge(att_done, done)
                row = xs[rows, bass.ds(tile, 1)].rearrange("p o (i l d) -> p (o l) i d", i=4, l=HQ)
                nc.vector.tensor_tensor(row, row, att[rows].rearrange("p (l i) d -> p l i d", i=4), ALU.add
                                        ).then_inc(x1_done, 1)

            def end_stats(tile, done):
                dve.wait_ge(x1_done, done)
                nc.vector.bn_stats(stats[:, 1, bass.ds(tile, 1)].rearrange("p o s -> p (o s)"),
                                   xs[:, bass.ds(tile, 1)].rearrange("p o d -> p (o d)")).then_inc(ln_stat, 1)

            def dve_step(T, k, pair):
                par, late = 1 - k // TILES, k % TILES
                tile, done = pair + (1 - par), pair * 2 + (k // TILES + 1)
                keys_ms(T + 3, k + 3)
                keys_spread(T + 1, k + 1)
                if late == 1:
                    end_columns(par, done)
                keys_norm(T + 2, k + 2)
                context_lo(T + 5, k + 5)
                keys_hi(T + 2, k + 2)
                keys_lo(T + 2, k + 2)
                if late == 2:
                    end_reciprocal(par, done)
                if late == 3:
                    end_weighted(par, done)
                if late == 4:
                    end_add(par, tile, done)
                if late == 5 and par:
                    end_stats(tile, done)

            context_lo(0, 0)
            dve.wait_ge(q_done, CHUNKS)
            nc.vector.memset(PV[:], 1.0).then_inc(pv_done, 1)
            dve.wait_ge(s_tanh, 1)
            context_lo(1, 1)
            for k in range(AHEAD_P):
                keys_ms(k, k)
                context_lo(k + 2, k + 2)
                if k > 1:
                    dve.wait_ge(lo_done, k - 1)
                if k > 0:
                    keys_norm(k - 1, k - 1)
                    keys_hi(k - 1, k - 1)
                    keys_lo(k - 1, k - 1)
            keys_spread(0, 0)
            dve_step(0, 0, 0)
            with dve.Fori(0, PAIRS) as pair:
                T0 = dve.snap(pair * PAIR_TILES)
                for k in range(1, PAIR_TILES + 1):
                    dve_step(T0 + k, k, pair)
            norm_variance(dve, 2)
            dve.wait_ge(sel_done, 1)
            nc.vector.tensor_copy(got[batch_rows(1), 0:SEL_XC], XC[batch_rows(1), 256:256 + SEL_XC])
            end_columns(1, B + 1)
            norm_root(dve, 2, 6 + 3 * CHUNKS)
            normed(xn2[:], 1, 0).then_inc(f_xn, 1)
            end_reciprocal(1, B + 1)
            end_weighted(1, B + 1)
            end_add(1, PAIRS, B + 1)
            end_stats(PAIRS, B + 1)
            norm_variance(dve, 3)
            ffn_vector(dve)

        @block.tensor
        def _(pe):
            pe.wait_ge(s_id, 4)

            def transpose_weights(banks, natural):
                for n, bank in enumerate(banks):
                    for c in range(IC):
                        for r in range(2):
                            tail = nc.tensor.transpose(bank[:, (c * 2 + r) * P:(c * 2 + r + 1) * P],
                                                       natural[:, 2 * n + r, c * P:c * P + P], ident[:])
                return tail

            pe.wait_ge(ld_q, 32)
            transpose_weights((S[:, 3],), wn_q)
            for c in range(IC):
                tail = nc.tensor.transpose(S[:, 2, c * FH:c * FH + FH], wn_g[:, c * P:c * P + P], ident[0:FH, 0:FH])
            tail.then_inc(wt_q, 1)
            pe.wait_ge(ld_kv, 32)
            transpose_weights((XK, PV), wn_kv[:].rearrange("p w r i -> p (w r) i")).then_inc(wt_kv, 1)
            def context_transpose(T, k):
                tile = k % TILES
                for c in range(IC):
                    tail = nc.tensor.transpose(x_ctx[:, c], cx[:, (k // TILES) % 2, tile, c * P:c * P + P], ident[:])
                tail.then_inc(t1_done, 1)

            def step(c, C):
                if c == CHUNKS:
                    pe.wait_ge(q_done, CHUNKS - 1)
                    pe.wait_ge(ld_pad, 32)
                    pe.wait_ge(ctx_loaded[0], 16)
                    context_transpose(0, 0)
                if is_chunk(c):
                    pe.wait_ge(ln_x, C + 1)
                    if c == 1:
                        pe.wait_ge(wc_act, 5)
                    for u in range(CT):
                        for k in range(IC):
                            tail = nc.tensor.transpose(S[:, c % 2, (u * IC + k) * P:(u * IC + k + 1) * P],
                                                       xn[:, c % 2, u, k * P:k * P + P], ident[:])
                    tail.then_inc(q_tr, 1)
                    pe.wait_ge(q_te, C + 1)
                    if c == 0:
                        pe.wait_ge(wc_act, 2)
                    if c >= 2:
                        pe.wait_ge(q_cp, C - 1)
                    for u in range(CT):
                        for k in range(IC):
                            tail = nc.tensor.matmul(S[:, 2 + c % 2, u * D:u * D + D], xn_t[:, c % 2, u, k],
                                                    wq_t[:, k], start=(k == 0), stop=(k == IC - 1))
                    tail.then_inc(q_mm, 1)
                if is_chunk(c - 1):
                    pe.wait_ge(q_lo, C)
                    if c == 2:
                        pe.wait_ge(wc_kv, 8)
                    if c >= 3:
                        pe.wait_ge(q_done, C - 2)
                    for u in range(CT):
                        for g in range(G):
                            tail = nc.tensor.transpose(part_banks(c - 1)[u][:].bitcast(F16)[:, g * P:g * P + P],
                                                       q4[:, (c - 1) % 2, u * G + g].rearrange("p a r -> p (a r)"),
                                                       ident16[:])
                    tail.then_inc(q_t4, 1)

            def after_first():
                pe.wait_ge(ld_qkv, 16)
                transpose_weights((S[:, 1], XC, Y), wn_qkv).then_inc(wt_qkv, 1)

            q_steps(pe, step, after_first)

            def project(k):
                steps = [(a, w, c) for a, w in ((cth, w_hi), (cth, w_lo), (ctl, w_hi)) for c in range(IC)]
                for n, (a, w, c) in enumerate(steps):
                    tail = nc.tensor.matmul(Y[:], a[:, k % 2, c], w[:, c].rearrange("p e h d -> p (e h d)"),
                                            start=(n == 0), stop=(n == len(steps) - 1))
                tail.then_inc(proj_done, 1)

            def key_transpose(T, k):
                for c in range(4):
                    tail = nc.tensor.transpose(x_key[:, c], kp[:, k % 2, 2 * c:2 * c + 2].rearrange(
                        "p g a r -> p (g a r)"), ident16[:])
                tail.then_inc(t2_done, 1)

            def score(par, half, done):
                for g in range(4 * half, 4 * half + 4):
                    tail = nc.tensor.matmul(S[:, g // 2, (g % 2) * 4 * N:(g % 2 + 1) * 4 * N], kt[:, g],
                                            q_bd[:, par, g].rearrange("p h n -> p (h n)"), start=True, stop=True)
                tail.then_inc(done, 1)

            def weigh(k):
                tile = k % TILES
                for at, heads in SLOTS:
                    for quad in range(4):
                        h = quad * HQ + at
                        tail = nc.tensor.matmul(PV[32 * quad:32 * quad + heads * VW, at * N:(at + heads) * N],
                                                v9[0:MT, k % VB, h * VW:(h + heads) * VW],
                                                prob[0:MT, k % 2, h * N:(h + heads) * N],
                                                start=(tile == 0 and at == 0), stop=(tile == TILES - 1),
                                                skip_group_check=True)
                if tile == TILES - 1:
                    tail.then_inc(pv_done, 1)

            def select(par, heads, bank):
                for n, h in enumerate(heads):
                    a = h - max(at for at, _ in SLOTS if at <= h)
                    tail = nc.tensor.matmul(
                        bank[batch_rows(par), 256 + n * SEL_W:256 + (n + 1) * SEL_W], pvs[:, h * N:(h + 1) * N],
                        ident[:].rearrange("p (i r) -> p i r", r=32)[:, :, a * VW:a * VW + VW],
                        start=True, stop=True)
                return tail

            for k in range(AHEAD_P):
                pe.wait_ge(ctl_ready, k + 1)
                context_transpose(k + 1, k + 1)
                if k > 0:
                    pe.wait_ge(y_free, k)
                project(k)
            pe.wait_ge(ctl_ready, 4)
            context_transpose(4, 4)
            pe.wait_ge(lo_done, 1)
            key_transpose(0, 0)

            def pe_step(T, k, pair):
                par = (k // TILES) % 2
                ended = k % TILES == 1
                pe.wait_ge(y_free, T + 3)
                project(k + 3)
                if k % TILES == 0:
                    pe.wait_ge(qbd_ready, (pair * 2 + (k // TILES + 1)) * G)
                pe.wait_ge(kt_ready, T + 1)
                pe.wait_ge(expa_done, T + 1)
                score(par, 0, sca_done)
                pe.wait_ge(expb_done, T + 1)
                score(par, 1, scb_done)
                if (k + AHEAD_T) % TILES == 0:
                    pe.wait_ge(ctx_loaded[1 - par], (pair + (1 + par)) * 16)
                pe.wait_ge(ctl_ready, T + 5)
                if ended:
                    pe.wait_ge(pvs_ready, pair * 2 + (k // TILES + 1))
                    select(1 - par, range(HQ - 1), XC)
                context_transpose(T + 5, k + 5)
                if ended:
                    select(1 - par, (HQ - 1,), XK)
                pe.wait_ge(lo_done, T + 2)
                key_transpose(T + 1, k + 1)
                if k > 0:
                    weigh(k - 1)

            pe_step(0, 0, 0)
            with pe.Fori(0, PAIRS) as pair:
                T0 = pe.snap(pair * PAIR_TILES)
                for k in range(1, PAIR_TILES + 1):
                    pe_step(T0 + k, k, pair)
            pe.wait_ge(pvs_ready, B + 1)
            pe.wait_ge(ctl_ready, B * TILES + AHEAD_T + 1)
            pe.wait_ge(kt_ready, B * TILES + 2)
            select(1, range(HQ - 1), XC)
            select(1, (HQ - 1,), XK).then_inc(sel_done, 1)
            ffn_tensor(pe)


_INS = ["x", "ctx_2048", "g_xattn", "g_ffn", "L0_xattn_Wq", "L0_xattn_Wk", "L0_xattn_Wv", "L0_ffn_W_gate",
        "L0_ffn_W_qkv"]


def kernel(**inputs):
    import numpy as _np
    import concourse.bacc as _bacc
    from concourse import mybir as _mybir
    from concourse.bass_utils import run_bass_kernel_spmd as _run

    nc = _bacc.Bacc("TRN2", target_bir_lowering=False, num_devices=1)
    arrays, args = {}, []
    for name in _INS:
        a = _np.ascontiguousarray(inputs[name])
        arrays[f"in_{name}_dram"] = a
        args.append(nc.dram_tensor(f"in_{name}_dram", a.shape, _mybir.dt.from_np(a.dtype), kind="ExternalInput").ap())
    args.append(nc.dram_tensor("out_0_dram", (B, N, D), _mybir.dt.float32, kind="ExternalOutput").ap())
    gated_attention_kernel(nc, *args)
    r = _run(nc, [arrays], core_ids=[0])
    return r.results[0]["out_0_dram"]
```
